# Optimizing a Trainium2 kernel written in Bass

```python
import numpy as np
import jax
import jax.numpy as jnp

def _softmax(x, axis=-1):
    return jax.nn.softmax(x, axis=axis)

def _gelu(x):
    return jax.nn.gelu(x, approximate=True)

def _silu(x):
    return jax.nn.silu(x)

def _sigmoid(x):
    return jax.nn.sigmoid(x)

def _layernorm(x, axis=-1, eps=1e-05):
    m = jnp.mean(x, axis=axis, keepdims=True)
    v = jnp.var(x, axis=axis, keepdims=True)
    return (x - m) / jnp.sqrt(v + eps)

def _scatter_add(tgt, idx, src, axis=0):
    return tgt.at[idx].add(src)

def _segment_sum(src, seg, n):
    return jax.ops.segment_sum(src, seg, n)
kernel_name = 'mk_flamingo_gated_d2_seqx_r4_f7d096'

def setup_inputs(seed: int=0):
    np.random.seed(seed)
    _w = jnp.asarray

    def _rec_inputs():
        import jax
        import jax.numpy as jnp
        _rk = jax.random.key(seed)
        x = -0.0003929 + 0.9999 * jax.random.normal(jax.random.fold_in(_rk, 1), (1, 2048, 256), jnp.float32)
        _lenS = 2048 - jax.random.randint(jax.random.fold_in(_rk, 7), (1,), 0, max(1, 2048 // 4) + 1, jnp.int32)
        _lenS2 = 1601 - jax.random.randint(jax.random.fold_in(_rk, 8), (1,), 0, max(1, 1601 // 4) + 1, jnp.int32)
        _ctx_2048P = jax.random.normal(jax.random.fold_in(_rk, 11), (1, 16, 512), jnp.float32)
        _ctx_2048c = jax.random.dirichlet(jax.random.fold_in(_rk, 511), 0.3 * jnp.ones((16,), jnp.float32), (1, 1601))
        _ctx_2048t = jnp.einsum('bsk,bkd->bsd', _ctx_2048c, _ctx_2048P)
        _ctx_2048t = _ctx_2048t * jax.lax.rsqrt(jnp.mean(jnp.square(_ctx_2048t)) + 1e-12) * 0.953939
        ctx_2048 = 4.13588e-05 + 0.999923 * (_ctx_2048t + 0.3 * jax.random.normal(jax.random.fold_in(_rk, 611), (1, 1601, 512), jnp.float32))
        _validS = jnp.arange(2048)[None, :] < _lenS[:, None]
        _validS2 = jnp.arange(1601)[None, :] < _lenS2[:, None]
        _causal = jnp.tril(jnp.ones((2048, 2048), dtype=bool))
        mask_BxS2_if0 = jnp.where(jnp.ones((1, 1601), dtype=bool), 4, 0).astype(jnp.int32)
        mask_BxS2_ik0 = jnp.where(jnp.broadcast_to(_validS2[:, :], (1, 1601)), 0, 1).astype(jnp.int32)
        _g = jax.random.normal(jax.random.fold_in(_rk, 9001), (2, 2), jnp.float32)
        _g = jnp.sign(_g) * jnp.maximum(jnp.abs(_g), 1.0) + (_g == 0) * 1.0
        g_xattn = _g[0]
        g_ffn = _g[1]
        return (x, ctx_2048, mask_BxS2_if0, mask_BxS2_ik0, g_xattn, g_ffn)
    x, ctx_2048, mask_BxS2_if0, mask_BxS2_ik0, g_xattn, g_ffn = _rec_inputs()

    def _L0_xattn_setup():
        import jax, jax.numpy as jnp
        import numpy as np
        B, L, P = (4, 1024, 256)
        D_MODEL = 256
        D_GLOBAL = 512
        HEADDIM = 32
        EPSILON = 0.001
        RMS_EPS = 1e-05

        def rmsnorm(x, g, eps=RMS_EPS):
            var = jnp.mean(jnp.square(x), axis=-1, keepdims=True)
            return x * jax.lax.rsqrt(var + eps) * g

        def _hnet_depool(h, h_patch_full, patch_lens):
            h_patch = h_patch_full[..., :D_MODEL]
            bsz, plen = (h_patch.shape[0], h_patch.shape[1])
            seqlen = h.shape[1]
            logp = jnp.full((bsz, plen), -EPSILON, dtype=jnp.float32)
            bidx = jnp.cumsum(patch_lens, axis=1) - 1
            boundary_mask = jnp.zeros((bsz, seqlen), dtype=jnp.int32)
            boundary_mask = boundary_mask.at[jnp.arange(bsz)[:, None], bidx].set(1)
            dt = (-jnp.log(-jnp.expm1(logp))).astype(h_patch.dtype)
            x = h_patch / dt[..., None]
            n_heads = D_MODEL // HEADDIM
            A = -jnp.ones((n_heads,), dtype=jnp.float32)
            bcoef = jnp.exp(logp).astype(h_patch.dtype)
            x4 = x.reshape(bsz, plen, n_heads, HEADDIM)
            a = jnp.exp(dt[:, :, None] * A[None, None, :])
            u = (dt * bcoef)[:, :, None, None] * x4
            a_b = jnp.broadcast_to(a[..., None], u.shape)

            def comb(lft, rgt):
                aL, uL = lft
                aR, uR = rgt
                return (aL * aR, uL * aR + uR)
            _, s = jax.lax.associative_scan(comb, (a_b, u), axis=1)
            depool = s.reshape(bsz, plen, D_MODEL)
            plug = jnp.clip(jnp.cumsum(boundary_mask, axis=1) - 1, 0, plen - 1)
            depool_out = depool[jnp.arange(bsz)[:, None], plug]
            return depool_out + h
        key = jax.random.key(seed)
        k1, k2, k3, k4 = jax.random.split(key, 4)
        embeds = jax.random.normal(k1, (B, L, D_MODEL), dtype=jnp.float32)
        patch_embeds = jax.random.normal(k2, (B, P, D_GLOBAL), dtype=jnp.float32)
        patch_lens = jnp.full((B, P), L // P, dtype=jnp.int64)
        W_in = jax.random.normal(k3, (D_MODEL, D_MODEL), dtype=jnp.float32) * 0.02
        b_in = jnp.zeros((D_MODEL,), dtype=jnp.float32)
        g_res = jnp.ones((D_MODEL,), dtype=jnp.float32)
        g_init = jnp.ones((D_GLOBAL,), dtype=jnp.float32)
        return {'embeds': embeds, 'patch_embeds': patch_embeds, 'patch_lens': patch_lens, 'W_in': W_in, 'b_in': b_in, 'g_res': g_res, 'g_init': g_init}
    _L0_xattn_all = _L0_xattn_setup()
    _L0_xattn_in = {k: v for k, v in _L0_xattn_all.items() if k in ('W_in', 'b_in', 'g_res', 'g_init')}
    del _L0_xattn_all

    def _L0_ffn_setup():
        import jax, jax.numpy as jnp
        import numpy as np
        B, S, DIM, FFN, E = (4, 512, 256, 1024, 8)
        key = jax.random.key(seed)
        k0, k1, k2, k3 = jax.random.split(key, 4)
        scale = 0.02
        return {'hidden_states': jax.random.normal(k0, (B, S, DIM), jnp.float32), 'router_w': jax.random.normal(k1, (DIM, E), jnp.float32) * scale, 'router_b': jnp.zeros((E,), jnp.float32), 'w1': jax.random.normal(k2, (E, DIM, 2 * FFN), jnp.float32) * scale, 'w2': jax.random.normal(k3, (E, FFN, DIM), jnp.float32) * scale}
    _L0_ffn_all = _L0_ffn_setup()
    _L0_ffn_in = {k: v for k, v in _L0_ffn_all.items() if k in ('router_w', 'router_b', 'w1', 'w2')}
    del _L0_ffn_all

    def _L1_xattn_setup():
        import jax, jax.numpy as jnp
        import numpy as np
        UNITS = 256
        NUM_HEADS = 8

        def _split_heads(x, n):
            B, S, D = x.shape
            return x.reshape(B, S, n, D // n).transpose(0, 2, 1, 3)
        key = jax.random.key(seed)
        k1, k2, k3 = jax.random.split(key, 3)
        B, S = (8, 256)
        memory = jax.random.normal(k1, (B, S, 2 * UNITS), dtype=jnp.float32)
        query = jax.random.normal(k2, (B, S, UNITS), dtype=jnp.float32)
        seq_mask = jax.random.randint(k3, (B, S), 0, 2, dtype=jnp.int32)
        b = jnp.zeros((1,), dtype=jnp.float32)
        return {'memory': memory, 'query': query, 'seq_mask': seq_mask, 'b': b}
    _L1_xattn_all = _L1_xattn_setup()
    _L1_xattn_in = {k: v for k, v in _L1_xattn_all.items() if k in ('b',)}
    del _L1_xattn_all

    def _L1_ffn_setup():
        import jax, jax.numpy as jnp
        import numpy as np
        EMB, HID, E, TOPK = (256, 1024, 8, 2)
        key = jax.random.key(seed)
        ks = jax.random.split(key, 10)
        s = 0.02
        return {'x': jax.random.normal(ks[0], (4, 512, EMB), jnp.float32), 'rw1': s * jax.random.normal(ks[1], (EMB, HID), jnp.float32), 'rb1': jnp.zeros((HID,), jnp.float32), 'rw2': s * jax.random.normal(ks[2], (HID, E), jnp.float32), 'rb2': jnp.zeros((E,), jnp.float32), 'w1': s * jax.random.normal(ks[3], (E, EMB, HID), jnp.float32), 'b1': jnp.zeros((E, HID), jnp.float32), 'w2': s * jax.random.normal(ks[4], (E, HID, EMB), jnp.float32), 'b2': jnp.zeros((E, EMB), jnp.float32)}
    _L1_ffn_all = _L1_ffn_setup()
    _L1_ffn_in = {k: v for k, v in _L1_ffn_all.items() if k in ('rw1', 'rb1', 'rw2', 'rb2', 'w1', 'b1', 'w2', 'b2')}
    del _L1_ffn_all
    return {'x': x, 'ctx_2048': ctx_2048, 'mask_BxS2_if0': mask_BxS2_if0, 'mask_BxS2_ik0': mask_BxS2_ik0, 'g_xattn': g_xattn, 'g_ffn': g_ffn, 'L0_xattn_W_in': _L0_xattn_in['W_in'], 'L0_xattn_b_in': _L0_xattn_in['b_in'], 'L0_xattn_g_res': _L0_xattn_in['g_res'], 'L0_xattn_g_init': _L0_xattn_in['g_init'], 'L0_ffn_router_w': _L0_ffn_in['router_w'], 'L0_ffn_router_b': _L0_ffn_in['router_b'], 'L0_ffn_w1': _L0_ffn_in['w1'], 'L0_ffn_w2': _L0_ffn_in['w2'], 'L1_xattn_b': _L1_xattn_in['b'], 'L1_ffn_rw1': _L1_ffn_in['rw1'], 'L1_ffn_rb1': _L1_ffn_in['rb1'], 'L1_ffn_rw2': _L1_ffn_in['rw2'], 'L1_ffn_rb2': _L1_ffn_in['rb2'], 'L1_ffn_w1': _L1_ffn_in['w1'], 'L1_ffn_b1': _L1_ffn_in['b1'], 'L1_ffn_w2': _L1_ffn_in['w2'], 'L1_ffn_b2': _L1_ffn_in['b2']}

def reference(x, ctx_2048, mask_BxS2_if0, mask_BxS2_ik0, g_xattn, g_ffn, L0_xattn_W_in, L0_xattn_b_in, L0_xattn_g_res, L0_xattn_g_init, L0_ffn_router_w, L0_ffn_router_b, L0_ffn_w1, L0_ffn_w2, L1_xattn_b, L1_ffn_rw1, L1_ffn_rb1, L1_ffn_rw2, L1_ffn_rb2, L1_ffn_w1, L1_ffn_b1, L1_ffn_w2, L1_ffn_b2):
    import jax
    import jax.numpy as jnp

    def _L0_xattn_ref(embeds, patch_embeds, patch_lens, W_in, b_in, g_res, g_init):
        import jax, jax.numpy as jnp
        import numpy as np
        B, L, P = (4, 1024, 256)
        D_MODEL = 256
        D_GLOBAL = 512
        HEADDIM = 32
        EPSILON = 0.001
        RMS_EPS = 1e-05

        def rmsnorm(x, g, eps=RMS_EPS):
            var = jnp.mean(jnp.square(x), axis=-1, keepdims=True)
            return x * jax.lax.rsqrt(var + eps) * g

        def _hnet_depool(h, h_patch_full, patch_lens):
            h_patch = h_patch_full[..., :D_MODEL]
            bsz, plen = (h_patch.shape[0], h_patch.shape[1])
            seqlen = h.shape[1]
            logp = jnp.full((bsz, plen), -EPSILON, dtype=jnp.float32)
            bidx = jnp.cumsum(patch_lens, axis=1) - 1
            boundary_mask = jnp.zeros((bsz, seqlen), dtype=jnp.int32)
            boundary_mask = boundary_mask.at[jnp.arange(bsz)[:, None], bidx].set(1)
            dt = (-jnp.log(-jnp.expm1(logp))).astype(h_patch.dtype)
            x = h_patch / dt[..., None]
            n_heads = D_MODEL // HEADDIM
            A = -jnp.ones((n_heads,), dtype=jnp.float32)
            bcoef = jnp.exp(logp).astype(h_patch.dtype)
            x4 = x.reshape(bsz, plen, n_heads, HEADDIM)
            a = jnp.exp(dt[:, :, None] * A[None, None, :])
            u = (dt * bcoef)[:, :, None, None] * x4
            a_b = jnp.broadcast_to(a[..., None], u.shape)

            def comb(lft, rgt):
                aL, uL = lft
                aR, uR = rgt
                return (aL * aR, uL * aR + uR)
            _, s = jax.lax.associative_scan(comb, (a_b, u), axis=1)
            depool = s.reshape(bsz, plen, D_MODEL)
            plug = jnp.clip(jnp.cumsum(boundary_mask, axis=1) - 1, 0, plen - 1)
            depool_out = depool[jnp.arange(bsz)[:, None], plug]
            return depool_out + h
        h = rmsnorm(embeds, g_res)
        h = jnp.einsum('bld,ed->ble', h, W_in) + b_in
        h_patch = rmsnorm(patch_embeds, g_init)
        return _hnet_depool(h, h_patch, patch_lens)

    def _L0_ffn_ref(hidden_states, router_w, router_b, w1, w2):
        import jax, jax.numpy as jnp
        import numpy as np
        B, S, DIM, FFN, E = (4, 512, 256, 1024, 8)
        b, s, d = hidden_states.shape
        x = hidden_states.reshape(-1, d)
        logits = x @ router_w + router_b
        route = jax.nn.softmax(logits, axis=1)
        max_prob = jnp.max(route, axis=1, keepdims=True)
        max_ind = jnp.argmax(route, axis=1)
        out = jnp.zeros_like(x)
        num_experts = w1.shape[0]
        for e in range(num_experts):
            h = x @ w1[e]
            a, g = jnp.split(h, 2, axis=1)
            y = jax.nn.silu(a) * g @ w2[e]
            out = jnp.where((max_ind == e)[:, None], y, out)
        out = out * max_prob
        return out.reshape(b, s, d)

    def _L1_xattn_ref(memory, query, seq_mask, b):
        import jax, jax.numpy as jnp
        import numpy as np
        UNITS = 256
        NUM_HEADS = 8

        def _split_heads(x, n):
            B, S, D = x.shape
            return x.reshape(B, S, n, D // n).transpose(0, 2, 1, 3)
        H = NUM_HEADS
        depth = UNITS // H
        Q = _split_heads(query, H) * depth ** (-0.5)
        k_mem, v_mem = jnp.split(memory, 2, axis=2)
        K = _split_heads(k_mem, H)
        V = _split_heads(v_mem, H)
        logits = jnp.einsum('bhqd,bhkd->bhqk', Q, K) + b[0]
        mask = seq_mask.astype(jnp.float32)[:, None, None, :]
        logits = logits + -1e+30 * (1.0 - mask)
        weights = jax.nn.softmax(logits, axis=-1)
        out = jnp.einsum('bhqk,bhkd->bhqd', weights, V)
        B, _, S, _ = out.shape
        return out.transpose(0, 2, 1, 3).reshape(B, S, UNITS)

    def _L1_ffn_ref(x, rw1, rb1, rw2, rb2, w1, b1, w2, b2):
        import jax, jax.numpy as jnp
        import numpy as np
        EMB, HID, E, TOPK = (256, 1024, 8, 2)
        B, S, D = x.shape
        logits = jax.nn.silu(jnp.einsum('bsd,dh->bsh', x, rw1) + rb1)
        logits = jnp.einsum('bsh,he->bse', logits, rw2) + rb2
        k_logits, k_index = jax.lax.top_k(logits, TOPK)
        k_prob = jax.nn.softmax(k_logits, axis=-1)
        xf = x.reshape(B * S, D)
        k_index_f = k_index.reshape(B * S, TOPK)
        k_prob_f = k_prob.reshape(B * S, TOPK)
        out = jnp.zeros_like(xf)
        for e in range(E):
            we = jnp.sum(jnp.where(k_index_f == e, k_prob_f, 0.0), axis=-1)
            h = jax.nn.silu(xf @ w1[e] + b1[e]) @ w2[e] + b2[e]
            out = out + we[:, None] * h
        return out.reshape(B, S, D)
    x = x + jnp.tanh(g_xattn[0]) * _L0_xattn_ref(_layernorm(x, axis=-1), ctx_2048, mask_BxS2_if0, L0_xattn_W_in, L0_xattn_b_in, L0_xattn_g_res, L0_xattn_g_init)
    x = x + jnp.tanh(g_ffn[0]) * _L0_ffn_ref(_layernorm(x, axis=-1), L0_ffn_router_w, L0_ffn_router_b, L0_ffn_w1, L0_ffn_w2)
    x = x + jnp.tanh(g_xattn[1]) * _L1_xattn_ref(ctx_2048, _layernorm(x, axis=-1), mask_BxS2_ik0, L1_xattn_b)
    x = x + jnp.tanh(g_ffn[1]) * _L1_ffn_ref(_layernorm(x, axis=-1), L1_ffn_rw1, L1_ffn_rb1, L1_ffn_rw2, L1_ffn_rb2, L1_ffn_w1, L1_ffn_b1, L1_ffn_w2, L1_ffn_b2)
    return x

_drawn_inputs = setup_inputs


def setup_inputs(seed=0):
    import zlib

    import numpy as np

    out = dict(_drawn_inputs(seed))
    spreads = {'g_ffn': (-1.0, 0.6),
     'L0_xattn_b_in': (0.0, 0.1),
     'L0_xattn_g_res': (1.0, 0.2),
     'L0_xattn_g_init': (1.0, 0.2),
     'L0_ffn_router_b': (0.0, 0.8),
     'L1_ffn_rb1': (0.0, 2.0),
     'L1_ffn_rb2': (0.0, 0.662),
     'L1_ffn_b1': (0.0, 2.0),
     'L1_ffn_b2': (0.0, 0.8)}
    factors = {'L0_ffn_router_w': 8.0,
     'L0_ffn_w1': 8.0,
     'L0_ffn_w2': 8.0,
     'L1_ffn_rw1': 8.0,
     'L1_ffn_rw2': 5.86,
     'L1_ffn_w1': 8.0,
     'L1_ffn_w2': 4.293}
    for name, (base, spread) in spreads.items():
        noise = np.random.default_rng([zlib.crc32(name.encode()), seed]).standard_normal(out[name].shape)
        drawn = base * np.exp(spread * noise) if base else spread * noise
        out[name] = jnp.asarray(drawn.astype(out[name].dtype))
    for name, factor in factors.items():
        out[name] = (out[name] * factor).astype(out[name].dtype)
    return out
```

```python
from contextlib import ExitStack

import numpy as np
import concourse.bass as bass
from concourse import mybir

F32 = mybir.dt.float32
F32R = mybir.dt.float32r
I32 = mybir.dt.int32
U32 = mybir.dt.uint32
BF16 = mybir.dt.bfloat16
ALU = mybir.AluOpType
ACT = mybir.ActivationFunctionType
AX = mybir.AxisListType

P = 128
D = 256
T = 2048
NC = T // P
S2 = 1601
NK = 13
REM = S2 - 12 * P
E = 8
FF = 1024
NT0 = T // P + E - 1
NT1 = 2 * T // P + E - 1
EPS = 1e-5
MASKED = -1e30
BEYOND = -3e38

C_ID, C_L, C_L2, C_U, C_ONE = 0, 128, 256, 384, 512
C_SEG, C_IO8, C_IOT, C_TP, C_SEG16 = 640, 896, 904, 944, 960
C_PAD = 1088
C_N = 1089
SMN = 2600


def constants():
    c = np.zeros((P, C_N), np.float32)
    dt = -np.log(-np.expm1(-0.001))
    a = np.exp(-dt)
    j = np.arange(P)
    gap = (j[None, :] - j[:, None]).astype(np.float64)
    c[:, C_ID:C_ID + P] = np.eye(P)
    c[:, C_L:C_L + P] = np.where(gap >= 0, np.power(a, np.maximum(gap, 0)), 0.0)
    c[:, C_L2:C_L2 + P] = np.power(a, np.minimum(gap + P, 60.0))
    c[:, C_U:C_U + P] = gap > 0
    c[:, C_ONE:C_ONE + P] = 1.0
    seg = np.ones((E, 32), np.float32)
    seg[:, 0] = 0.0
    c[:, C_SEG:C_SEG + E * 32] = seg.reshape(-1)
    c[:, C_SEG16:C_SEG16 + E * 16] = seg[:, :16].reshape(-1)
    c[:, C_IO8:C_IO8 + E] = np.arange(E)
    c[:, C_IOT:C_IOT + 40] = np.arange(40)
    c[:, C_TP:C_TP + NC] = np.arange(NC)[None, :] * P + j[:, None] + 1
    c[REM:, C_PAD] = BEYOND
    return c


class Queue:

    def __init__(self, sem):
        self.sem, self.n, self.ops, self.seen = sem, 0, [], {}

    def do(self, make, count=True):
        if count:
            self.n += 1
            self.ops.append(lambda e: make(e).then_inc(self.sem, 1))
            return (self.sem, self.n)
        self.ops.append(make)
        return None

    def on(self, *tokens):
        for token in tokens:
            if token is None:
                continue
            sem, n = token
            if self.seen.get(sem.name, 0) < n:
                self.seen[sem.name] = n
                self.ops.append(lambda e, sem=sem, n=n: e.wait_ge(sem, n))

    def dma(self, dsem, make):
        dsem.n += 16
        self.ops.append(lambda e: make(e).then_inc(dsem.sem, 16))
        return (dsem.sem, dsem.n)

    def play(self, e):
        for op in self.ops:
            op(e)


class DmaSem:
    def __init__(self, sem):
        self.sem, self.n = sem, 0


def build(nc, cst, x, ctx_2048, plen, kmask, g_xattn, g_ffn, W_in, b_in, g_res, g_init, rw0, rb0, w01, w02,
          att_b, rw1, rb1, rw2, rb2, w11, b11, w12, b12, out):
    es = ExitStack()
    with es:
        def sb(name, shape, dt=F32):
            return es.enter_context(nc.sbuf_tensor(name, shape, dt))[:, :]

        def queue(name):
            return Queue(es.enter_context(nc.semaphore(name)))

        def dsem(name):
            return DmaSem(es.enter_context(nc.semaphore(name)))

        sp, pe, ac, ve, po = (queue(n) for n in ("q_sp", "q_pe", "q_ac", "q_ve", "q_po"))

        X = sb("X", [P, NC * D]).rearrange("p (c d) -> p c d", d=D)
        WS = [sb(f"WS{i}", [P, 6144]) for i in range(2)]
        KS = sb("KS", [P, E * NK * P], F32R).rearrange("p (h k) -> p h k", h=E)
        V = sb("V", [P, NK * D]).rearrange("p (c d) -> p c d", d=D)
        Z0 = sb("Z0", [P, 4096])
        Z1 = sb("Z1", [P, 4096])
        QS = [sb(f"QS{i}", [P, 2048], F32R).rearrange("p (h q) -> p h q", h=4) for i in range(2)]
        AK = [sb(f"AK{i}", [P, 1024], F32R).rearrange("p (h c) -> p h c", h=8) for i in range(2)]
        AU = [sb(f"AU{i}", [P, 512], F32R).rearrange("p (h c) -> p h c", h=4) for i in range(2)]
        MBH = sb("MBH", [P, 2 * NK], F32R)
        CT = sb("CT", [P, C_N])
        SM = sb("SM", [P, SMN])
        SI = sb("SI", [P, 128], I32)
        CK = Z1[:, 0:NK * D].rearrange("p (c d) -> p c d", d=D)
        PQ = es.enter_context(nc.psum_tensor("PQ", [P, 2048], F32))[:, :]
        PB = [PQ[:, 512 * i:512 * i + 512] for i in range(4)]
        PB += [es.enter_context(nc.psum_tensor(f"PB{i}", [P, 512], F32))[:, :] for i in range(4, 8)]

        def scratch(name, rows):
            return nc.dram_tensor(name, [rows, D], F32, kind="Internal").ap()

        dep_d, xs0, ys0, xs1, ys1 = (scratch(n, r) for n, r in (
            ("dep_d", NK * P), ("xs0", NT0 * P), ("ys0", NT0 * P), ("xs1", NT1 * P), ("ys1", NT1 * P)))

        at = [0]

        def sm(n):
            at[0] += n
            assert at[0] <= SMN, at[0]
            return SM[:, at[0] - n:at[0]]

        ident, ones = CT[:, C_ID:C_ID + P], CT[:, C_ONE:C_ONE + P]
        gates, tg, attb, gres = sm(4), sm(4), sm(1), sm(2)
        rw0s, rb0s, rb1s, rw2s, rb2s = sm(16), sm(8), sm(8), sm(64), sm(8)
        ssk, ssv, rs, mb = sm(NK), sm(NK), sm(NK), sm(NK)
        st6, mv, rst, rst2, nh = sm(NC * 6), sm(NC * 2), sm(NC), sm(NC), sm(16)
        flag = sm(4)
        lg, la, OH = sm(NC * E), sm(NC * E), sm(2 * NC * E)
        inc, rk = sm(2 * NC * E), sm(2 * NC * E)
        m1, m2, pr, tt, pos = sm(NC), sm(NC), sm(2 * NC), sm(NC), sm(2 * NC)
        cnt, nti, bi, bas = sm(E), sm(E), sm(E), sm(E)
        b1c = [sm(8), sm(8)]
        mxx, sc7 = sm(80), sm(280)
        plugi, posi, eidi, ntii, mski = SI[:, 0:16], SI[:, 16:48], SI[:, 48:88], SI[:, 88:96], SI[:, 96:109]

        d_c, d_s, d_p, d_k, d_v, d_x = (dsem(n) for n in ("d_c", "d_s", "d_p", "d_k", "d_v", "d_x"))
        Win = Z0[:, 0:512].rearrange("p (k n) -> p k n", k=2)
        gIB, bIB = Z0[:, 512:768], Z0[:, 768:1024]
        U3 = [Z0[:, 1024 + 256 * i:1280 + 256 * i] for i in range(3)]
        DR = [Z0[:, 1792 + 256 * i:2048 + 256 * i] for i in range(2)]
        junk = Z0[:, 2304:2304 + 1602]
        plrow = WS[0][0:1, 0:1601].bitcast(I32)
        plf = WS[0][0:1, 1602:3204]
        cum = WS[0][0:1, 3204:4806]
        lz = WS[0][0:1, 4806:4816]
        rowt = Z0[0:1, 2304:2304 + 1601]

        def load(q, d, dst, src):
            return q.dma(d, lambda e: e.dma_start(dst, src))

        load(sp, d_p, plrow, plen)
        for c in range(0, NC, 4):
            t_x = load(sp, d_x, X[:, c:c + 4, :], x[c * P:(c + 4) * P, :].rearrange("(c p) d -> p c d", p=P))
        t_mz = ve.do(lambda e: e.memset(CK[:, 12, :], 0.0))
        t_vz = ve.do(lambda e: e.memset(V[:, 12, :], 0.0))
        t_p = (d_p.sem, 16)
        load(ac, d_c, CT, cst)
        t_c = (d_c.sem, 16)
        load(ac, d_k, CK[:, 0:12, :], ctx_2048[0:12 * P, 0:D].rearrange("(c p) d -> p c d", p=P))
        ac.on(t_mz, t_vz)
        load(ac, d_k, CK[0:REM, 12, :], ctx_2048[12 * P:S2, 0:D])
        load(ac, d_k, V[:, 0:12, :], ctx_2048[0:12 * P, D:2 * D].rearrange("(c p) d -> p c d", p=P))
        load(ac, d_k, V[0:REM, 12, :], ctx_2048[12 * P:S2, D:2 * D])
        t_k = load(ac, d_k, mski, kmask)
        load(sp, d_s, gIB, g_init[:, 0:D].partition_broadcast(P))
        load(sp, d_s, bIB, b_in.partition_broadcast(P))
        load(sp, d_s, Win, W_in.rearrange("(k p) n -> p k n", p=P))
        load(sp, d_s, gres, g_res)
        load(sp, d_s, gates[:, 0:2], g_xattn.partition_broadcast(P))
        load(sp, d_s, gates[:, 2:4], g_ffn.partition_broadcast(P))
        load(sp, d_s, attb, att_b.partition_broadcast(P))
        load(sp, d_s, rw0s.rearrange("p (k n) -> p k n", k=2), rw0.rearrange("(k p) n -> p k n", p=P))
        load(sp, d_s, rb0s, rb0.partition_broadcast(P))
        load(sp, d_s, rb1s, rb1)
        load(sp, d_s, rw2s.rearrange("p (k n) -> p k n", k=8), rw2.rearrange("(k p) n -> p k n", p=P))
        t_s = load(sp, d_s, rb2s, rb2.partition_broadcast(P))

        zero = WS[1][:, 3072:5120]
        t_z = po.do(lambda e: e.memset(zero, 0.0))
        po.do(lambda e: e.memset(nh, -0.5))
        d_z = dsem("d_z")
        ac.on(t_z)
        for buf, nt in ((xs0, NT0), (xs1, NT1)):
            v = buf.rearrange("(p r) d -> p (r d)", p=P)
            for r in range(0, nt, 8):
                k = min(8, nt - r)
                t_zero = load(ac, d_z, v[:, r * D:(r + k) * D], zero[:, 0:k * D])
        for t in AK + AU:
            po.do(lambda e, t=t: e.memset(t[:, :, 96:128].bitcast(F32), 0.0))
        for t in AU:
            po.do(lambda e, t=t: e.memset(t[:, :, 0:96].bitcast(F32), 0.0))
        po.on((po.sem, po.n))
        for t in AU:
            po.do(lambda e, t=t: e.memset(t[:, :, 96:97].bitcast(F32), 1.0))
            t_au = po.do(lambda e, t=t: e.memset(t[:, :, 98:99].bitcast(F32), 1.0))
        for t in AK:
            po.do(lambda e, t=t: e.memset(t[:, :, 97:98].bitcast(F32), 1.0))
            t_au = po.do(lambda e, t=t: e.memset(t[:, :, 99:100].bitcast(F32), 1.0))

        ac.on(t_s)
        t_tg = ac.do(lambda e: e.activation(tg, gates, ACT.Tanh))

        def link(q, make):
            t = q.do(make)
            q.on(t)
            return t

        ve.on(t_p, t_c, t_s)
        link(ve, lambda e: e.tensor_scalar(plf[:, 0:S2], plrow, 4096.0, None, ALU.min))
        link(ve, lambda e: e.tensor_tensor_scan(cum[:, 0:S2], CT[0:1, C_ONE:C_ONE + 1].broadcast_to([1, S2]),
                                                plf[:, 0:S2], 0.0, ALU.mult, ALU.add))
        link(ve, lambda e: e.tensor_single_scalar(plf[:, 0:S2], plf[:, 0:S2], 0.0, ALU.is_equal))
        link(ve, lambda e: e.scalar_tensor_tensor(cum[:, 0:S2], plf[:, 0:S2], 4.0e6, cum[:, 0:S2], ALU.mult, ALU.add))
        link(ve, lambda e: e.tensor_single_scalar(rowt, cum[:, 0:S2], float(T), ALU.is_equal))
        link(ve, lambda e: e.tensor_reduce(lz[:, 0:1], rowt, AX.X, ALU.max))
        link(ve, lambda e: e.tensor_scalar(lz[:, 1:2], lz[:, 0:1], -1.0, 1.0, ALU.mult, ALU.add))
        link(ve, lambda e: e.tensor_tensor(lz[:, 2:3], lz[:, 1:2], plf[:, 0:1], ALU.mult))
        t_cum = link(ve, lambda e: e.tensor_scalar(cum[:, S2:S2 + 1], lz[:, 2:3], float(T) - 4.0e6, 4.0e6, ALU.mult, ALU.add))
        pe.on(t_cum, t_c)
        for i, (a, b) in enumerate(((0, 512), (512, 1024), (1024, 1536), (1536, 1602))):
            t_cb = pe.do(lambda e, i=i, a=a, b=b: e.matmul(PB[i][:, 0:b - a], CT[0:1, C_ONE:C_ONE + P], cum[:, a:b],
                                                           start=True, stop=True))
        ve.on(t_cb)

        for c in range(NC):
            link(ve, lambda e, c=c: e.tensor_scalar(junk, PQ[:, 0:1602], CT[:, C_TP + c:C_TP + c + 1], 0.0, ALU.is_le,
                                                    ALU.add, accum_out=pos[:, c:c + 1]))
        t_pq = (ve.sem, ve.n)
        link(ve, lambda e: e.tensor_scalar(tt, pos[:, 0:NC], 1.0, float(S2), ALU.subtract, ALU.min))
        link(ve, lambda e: e.tensor_scalar(tt, tt, float(S2 - 1), 0.0, ALU.min, ALU.max))
        t_plug = link(ve, lambda e: e.tensor_copy(plugi, tt))

        ve.on(t_k)
        ac.on(t_k, t_mz, t_vz)
        for c in range(NK):
            ac.do(lambda e, c=c: e.activation(PB[4][:, 0:D], CK[:, c, :], ACT.Square, accum_out=ssk[:, c:c + 1]))
            t_ss = ac.do(lambda e, c=c: e.activation(PB[5][:, 0:D], V[:, c, :], ACT.Square, accum_out=ssv[:, c:c + 1]))
            ac.on(t_ss)
        ve.on(t_ss)
        link(ve, lambda e: e.tensor_tensor(rs, ssk, ssv, ALU.add))
        t = link(ve, lambda e: e.tensor_scalar(rs, rs, 1.0 / (2 * D), EPS, ALU.mult, ALU.add))
        po.on(t)
        t = link(po, lambda e: e.tensor_tensor(rs, rs, nh[:, 0:NK], ALU.pow))
        ve.on(t)
        link(ve, lambda e: e.tensor_scalar(rs, rs, float(np.float32(np.exp(-0.001))), None, ALU.mult))

        d_dr = [dsem(f"d_dr{i}") for i in range(2)]
        t_u, t_sc, t_dr = [], [], []
        def evac_dep(c):
            ve.on(t_sc[c])
            if c >= 2:
                ve.on(t_dr[c - 2])
            t = ve.do(lambda e: e.tensor_tensor(DR[c % 2], PB[6 + c % 2][:, 0:D], bIB, ALU.add))
            sp.on(t)
            t_dr.append(load(sp, d_dr[c % 2], dep_d[c * P:(c + 1) * P, :], DR[c % 2]))
            return t

        for c in range(NK):
            if c >= 3:
                ve.on(t_sc[c - 2])
            t_u.append(ve.do(lambda e, c=c: e.scalar_tensor_tensor(U3[c % 3], CK[:, c, :], rs[:, c:c + 1], gIB,
                                                                   ALU.mult, ALU.mult)))
            bank = PB[6 + c % 2][:, 0:D]
            pe.on(t_u[c])
            if c >= 2:
                pe.on(t_ev)
            pe.do(lambda e, c=c, bank=bank: e.matmul(bank, CT[:, C_L:C_L + P], U3[c % 3], start=True, stop=c == 0),
                  count=c == 0)
            if c:
                pe.do(lambda e, c=c, bank=bank: e.matmul(bank, CT[:, C_L2:C_L2 + P], U3[(c - 1) % 3],
                                                         start=False, stop=True))
            t_sc.append((pe.sem, pe.n))
            if c >= 1:
                t_ev = evac_dep(c - 1)
        t_ev = evac_dep(NK - 1)

        def stats(c, after=None):
            ve.on(after)
            t = ve.do(lambda e: e.bn_stats(st6[:, 6 * c:6 * c + 6], X[:, c, :]))
            ve.on(t)
            return ve.do(lambda e: e.bn_aggr(mv[:, 2 * c:2 * c + 2], st6[:, 6 * c:6 * c + 6]))

        mean = mv.rearrange("p (c s) -> p c s", s=2)[:, :, 0]
        var = mv.rearrange("p (c s) -> p c s", s=2)[:, :, 1]

        def inv_std(after):
            ve.on(after)
            t = ve.do(lambda e: e.tensor_scalar(rst, var, EPS, None, ALU.add))
            po.on(t)
            t = po.do(lambda e: e.tensor_tensor(rst, rst, nh, ALU.pow))
            ve.on(t)
            return t

        ve.on((d_x.sem, 64))
        for c in range(NC):
            t = stats(c)
        inv_std(t)
        link(ve, lambda e: e.tensor_tensor(rst2, rst, rst, ALU.mult))
        link(ve, lambda e: e.tensor_tensor(rst2, rst2, var, ALU.mult))
        t = link(ve, lambda e: e.tensor_scalar(rst2, rst2, EPS, None, ALU.add))
        po.on(t)
        t = link(po, lambda e: e.tensor_tensor(rst2, rst2, nh, ALU.pow))
        ve.on(t)
        link(ve, lambda e: e.tensor_tensor(rst2, rst2, rst, ALU.mult))
        for k in range(2):
            t_win = ve.do(lambda e, k=k: e.tensor_scalar(Win[:, k, :], Win[:, k, :], gres[:, k:k + 1], None, ALU.mult))

        HIN = [WS[1][:, 256 * i:256 * i + 256] for i in range(4)]
        HT = [WS[1][:, 1024 + 256 * i:1280 + 256 * i] for i in range(4)]
        DG = [WS[1][:, 2048 + 256 * i:2304 + 256 * i] for i in range(4)]
        d_dg = [dsem(f"d_dg{i}") for i in range(4)]
        t_hin, t_tr, t_ht, t_mm, t_dg, t_x1, t_st = {}, {}, {}, {}, {}, {}, {}

        po.on(t_plug, *t_dr[-2:])
        for c in range(NC + 2):
            if c < NC:
                if c >= 4:
                    po.on(t_x1[c - 4])
                t_dg[c] = po.dma(d_dg[c % 4], lambda e, c=c: e.indirect_dma_start(
                    DG[c % 4], None, dep_d, bass.IndirectOffsetOnAxis(ap=plugi[:, c:c + 1].bitcast(U32), axis=0)))
                if c >= 4:
                    ve.on(t_tr[c - 4])
                t_hin[c] = ve.do(lambda e, c=c: e.tensor_scalar(HIN[c % 4], X[:, c, :], mean[:, c:c + 1],
                                                                rst2[:, c:c + 1], ALU.subtract, ALU.mult))
                pe.on(t_hin[c], t_pq, t_ss, t_ht.get(c - 2))
                for k in range(2):
                    t_tr[c] = pe.do(lambda e, c=c, k=k: e.transpose(PB[4 + c % 2][:, k * P:k * P + P],
                                                                    HIN[c % 4][:, k * P:k * P + P], ident))
                ac.on(t_tr[c], t_mm.get(c - 4))
                t_ht[c] = ac.do(lambda e, c=c: e.activation(HT[c % 4], PB[4 + c % 2][:, 0:D], ACT.Copy))
            b = c - 1
            if 0 <= b < NC:
                pe.on(t_ht[b], t_win, t_ev, t_x1.get(b - 2))
                for k in range(2):
                    t_mm[b] = pe.do(lambda e, b=b, k=k: e.matmul(PB[6 + b % 2][:, 0:D], HT[b % 4][:, k * P:k * P + P],
                                                                 Win[:, k, :], start=k == 0, stop=k == 1))
            b = c - 2
            if 0 <= b < NC:
                ve.on(t_mm[b], t_dg[b], t_tg)
                t = ve.do(lambda e, b=b: e.tensor_tensor(DG[b % 4], PB[6 + b % 2][:, 0:D], DG[b % 4], ALU.add))
                ve.on(t)
                t_x1[b] = ve.do(lambda e, b=b: e.scalar_tensor_tensor(X[:, b, :], DG[b % 4], tg[:, 0:1], X[:, b, :],
                                                                      ALU.mult, ALU.add))
                t_st[b] = stats(b, t_x1[b])

        def cols(v, n):
            return v.rearrange("p (c e) -> p c e", e=n)

        def route(picks, logits_at, rb, nt, after):
            cc = NC * picks
            l3, a3 = cols(lg, E), cols(la, E)
            ve.on(after)
            link(ve, lambda e: e.tensor_tensor(l3, logits_at, rb.unsqueeze(1).broadcast_to([P, NC, E]), ALU.add))
            iota = CT[:, C_IO8:C_IO8 + E].unsqueeze(1).broadcast_to([P, NC, E])
            oh = OH[:, 0:E * cc].rearrange("p (e c) -> p c e", e=E)

            def pick(k, m):
                link(ve, lambda e: e.tensor_reduce(m, l3, AX.X, ALU.max))
                link(ve, lambda e: e.tensor_tensor(a3, l3, m.unsqueeze(2).broadcast_to([P, NC, E]), ALU.is_lt))
                link(ve, lambda e: e.scalar_tensor_tensor(a3, a3, 100.0, iota, ALU.mult, ALU.add))
                link(ve, lambda e: e.tensor_reduce(tt, a3, AX.X, ALU.min))
                link(ve, lambda e: e.tensor_tensor(oh[:, k * NC:(k + 1) * NC, :], iota,
                                                   tt.unsqueeze(2).broadcast_to([P, NC, E]), ALU.is_equal))

            pick(0, m1)
            if picks == 1:
                t = link(ve, lambda e: e.tensor_tensor(a3, l3, m1.unsqueeze(2).broadcast_to([P, NC, E]), ALU.subtract))
                ac.on(t)
                t = ac.do(lambda e: e.activation(la, la, ACT.Exp))
                ve.on(t)
                link(ve, lambda e: e.tensor_reduce(pr[:, 0:NC], a3, AX.X, ALU.add))
                link(ve, lambda e: e.reciprocal(pr[:, 0:NC], pr[:, 0:NC]))
            else:
                link(ve, lambda e: e.scalar_tensor_tensor(l3, oh[:, 0:NC, :], -3.0e38, l3, ALU.mult, ALU.add))
                pick(1, m2)
                t = link(ve, lambda e: e.tensor_tensor(tt, m2, m1, ALU.subtract))
                ac.on(t)
                t = ac.do(lambda e: e.activation(tt, tt, ACT.Exp))
                ve.on(t)
                link(ve, lambda e: e.tensor_scalar(m1, tt, 1.0, None, ALU.add))
                link(ve, lambda e: e.reciprocal(pr[:, 0:NC], m1))
                link(ve, lambda e: e.tensor_tensor(pr[:, NC:2 * NC], pr[:, 0:NC], tt, ALU.mult))
            gate = 2 if picks == 1 else 3
            link(ve, lambda e: e.tensor_scalar(pr[:, 0:cc], pr[:, 0:cc], tg[:, gate:gate + 1], None, ALU.mult))
            n = E * cc
            pe.on((ve.sem, ve.n))
            pe.do(lambda e: e.matmul(PB[4][:, 0:n], CT[:, C_U:C_U + P], OH[:, 0:n], start=True, stop=True))
            t = pe.do(lambda e: e.matmul(PB[5][:, 0:n], ones, OH[:, 0:n], start=True, stop=True))
            ve.on(t)
            seg = CT[:, C_SEG:C_SEG + n] if picks == 2 else CT[:, C_SEG16:C_SEG16 + n]
            link(ve, lambda e: e.tensor_tensor_scan(inc[:, 0:n], seg, PB[5][:, 0:n], 0.0, ALU.mult, ALU.add))
            link(ve, lambda e: e.tensor_tensor(rk[:, 0:n], inc[:, 0:n], PB[5][:, 0:n], ALU.subtract))
            link(ve, lambda e: e.tensor_tensor(rk[:, 0:n], rk[:, 0:n], PB[4][:, 0:n], ALU.add))
            last = inc[:, 0:n].rearrange("p (e c) -> p e c", e=E)[:, :, cc - 1]
            link(ve, lambda e: e.tensor_scalar(ntii, last, float(P - 1), None, ALU.add))
            link(ve, lambda e: e.tensor_single_scalar(ntii, ntii, 7, ALU.arith_shift_right))
            link(ve, lambda e: e.tensor_scalar(nti, ntii, 1.0, None, ALU.max))
            link(ve, lambda e: e.tensor_tensor_scan(bi, ones[:, 0:E], nti, 0.0, ALU.mult, ALU.add))
            link(ve, lambda e: e.tensor_tensor(bas, bi, nti, ALU.subtract))
            link(ve, lambda e: e.tensor_scalar(bas, bas, float(P), None, ALU.mult))
            r3 = rk[:, 0:n].rearrange("p (e c) -> p e c", e=E)
            link(ve, lambda e: e.tensor_tensor(r3, r3, bas.unsqueeze(2).broadcast_to([P, E, cc]), ALU.add))
            link(ve, lambda e: e.tensor_tensor(rk[:, 0:n], rk[:, 0:n], OH[:, 0:n], ALU.mult))
            link(ve, lambda e: e.tensor_reduce(pos[:, 0:cc], rk[:, 0:n].rearrange("p (e c) -> p c e", e=E), AX.X, ALU.add))
            t_pos = link(ve, lambda e: e.tensor_copy(posi[:, 0:cc], pos[:, 0:cc]))
            b7 = sc7[:, 0:nt * 7].rearrange("p (t e) -> p t e", e=7)
            link(ve, lambda e: e.tensor_tensor(b7, CT[:, C_IOT:C_IOT + nt].unsqueeze(2).broadcast_to([P, nt, 7]),
                                               bi[:, 0:7].unsqueeze(1).broadcast_to([P, nt, 7]), ALU.is_ge))
            link(ve, lambda e: e.tensor_reduce(mxx[:, 0:nt], b7, AX.X, ALU.add))
            t_eid = link(ve, lambda e: e.tensor_copy(eidi[:, 0:nt], mxx[:, 0:nt]))
            return t_pos, t_eid


        def scatter(c, xnt, xs, t_xn, picks, dst, free):
            po.on(t_xn)
            for k in range(picks):
                j = k * NC + c
                t = po.dma(dst, lambda e, j=j: e.indirect_dma_start(
                    xs, bass.IndirectOffsetOnAxis(ap=posi[:, j:j + 1].bitcast(U32), axis=0), xnt, None))
            return t

        XN = [WS[1][:, 256 * i:256 * i + 256] for i in range(4)]
        XT = [WS[1][:, 1024 + 256 * i:1280 + 256 * i] for i in range(4)]
        inv_std(t_st[NC - 1])
        t_xn, t_tr, t_xt, t_mm = {}, {}, {}, {}
        for c in range(NC + 1):
            if c < NC:
                ve.on(t_tr.get(c - 4))
                t_xn[c] = ve.do(lambda e, c=c: e.tensor_scalar(XN[c % 4], X[:, c, :], mean[:, c:c + 1],
                                                               rst[:, c:c + 1], ALU.subtract, ALU.mult))
                pe.on(t_xn[c], t_xt.get(c - 2))
                for k in range(2):
                    t_tr[c] = pe.do(lambda e, c=c, k=k: e.transpose(PB[4 + c % 2][:, k * P:k * P + P],
                                                                    XN[c % 4][:, k * P:k * P + P], ident))
                ac.on(t_tr[c], t_mm.get(c - 4))
                t_xt[c] = ac.do(lambda e, c=c: e.activation(XT[c % 4], PB[4 + c % 2][:, 0:D], ACT.Copy))
            b = c - 1
            if 0 <= b < NC:
                pe.on(t_xt[b], t_x1[NC - 1])
                for k in range(2):
                    t_mm[b] = pe.do(lambda e, b=b, k=k: e.matmul(PB[6][:, b * E:b * E + E],
                                                                 XT[b % 4][:, k * P:k * P + P],
                                                                 rw0s[:, k * E:k * E + E], start=k == 0, stop=k == 1))
        t_pos, t_eid = route(1, PB[6][:, 0:NC * E].rearrange("p (c e) -> p c e", e=E), rb0s, NT0, t_mm[NC - 1])

        d_sc = [dsem(f"d_sc{i}") for i in range(4)]
        t_sct = {}
        po.on(t_pos, t_zero)
        for c in range(NC):
            ve.on(t_tr[NC - 1], t_sct.get(c - 4))
            t = ve.do(lambda e, c=c: e.tensor_scalar(XN[c % 4], X[:, c, :], mean[:, c:c + 1],
                                                     rst[:, c:c + 1], ALU.subtract, ALU.mult))
            t_sct[c] = scatter(c, XN[c % 4], xs0, t, 1, d_sc[c % 4], None)
        t_scat = [t_sct[c] for c in range(NC - 4, NC)]

        ve.on(t_k)
        link(ve, lambda e: e.tensor_scalar(mb[:, 0:NK], mski, -MASKED, MASKED, ALU.mult, ALU.add))
        link(ve, lambda e: e.tensor_scalar(mb[:, 0:NK], mb[:, 0:NK], attb[:, 0:1], None, ALU.add))
        link(ve, lambda e: e.tensor_tensor(mb[:, 12:13], mb[:, 12:13], CT[:, C_PAD:C_PAD + 1], ALU.add))
        link(ve, lambda e: e.tensor_copy(MBH[:, 0:NK], mb))
        t_mbh = link(ve, lambda e: e.tensor_tensor(MBH[:, NK:2 * NK], mb, MBH[:, 0:NK].bitcast(F32), ALU.subtract))
        link(ve, lambda e: e.tensor_copy(ssk, mski))
        t = link(ve, lambda e: e.tensor_reduce(flag[:, 0:1], ssk, AX.X, ALU.max))
        pe.on(t)
        t = pe.do(lambda e: e.matmul(PB[4][0:1, 0:P], flag[:, 0:1], ident, start=True, stop=True))
        ve.on(t)
        t = link(ve, lambda e: e.tensor_reduce(flag[0:1, 1:2], PB[4][0:1, 0:P], AX.X, ALU.max))
        pe.on(t)
        t = pe.do(lambda e: e.matmul(PB[4][:, 0:1], CT[0:1, C_ONE:C_ONE + P], flag[0:1, 1:2], start=True, stop=True))
        ve.on(t)
        t_flag = link(ve, lambda e: e.tensor_scalar(flag[:, 2:3], PB[4][:, 0:1], 32.0 ** -0.5, None, ALU.mult))

        t_kst, t_kev = {}, []

        def keys_a(c):
            a = AK[c % 2]
            k3 = CK[:, c, :].rearrange("p (h d) -> p h d", h=E)
            ve.on(t_kst.get(c - 2), t_au, t_mbh)
            t = ve.do(lambda e: e.tensor_copy(a[:, :, 0:32], k3))
            ve.do(lambda e: e.tensor_copy(a[:, :, 32:64], k3))
            for j, o in ((0, 96), (1, 98)):
                ve.do(lambda e, j=j, o=o: e.tensor_copy(
                    a[:, :, o:o + 1],
                    MBH[:, j * NK + c:j * NK + c + 1].bitcast(F32).unsqueeze(1).broadcast_to([P, E, 1])))
            ve.on(t)
            return ve.do(lambda e: e.tensor_tensor(a[:, :, 64:96], k3, a[:, :, 0:32].bitcast(F32), ALU.subtract))

        t_trf = [t_flag, t_flag]
        trn = [0]

        def turn(ins, after, evac, free=None):
            j = trn[0] % 2
            trn[0] += 1
            bank = PB[4 + j]
            pe.on(*after, t_trf[j])
            for i, v in enumerate(ins):
                t = pe.do(lambda e, i=i, v=v: e.transpose(bank[:, i * P:i * P + P], v, ident), count=i == len(ins) - 1)
            t_trf[j] = evac(bank, t)
            return t, t_trf[j]

        d_w1 = [dsem(f"d_w1{i}") for i in range(2)]
        d_w2 = [dsem(f"d_w2{i}") for i in range(2)]
        d_b = [dsem(f"d_b{i}") for i in range(2)]
        d_xl = [dsem(f"d_xl{i}") for i in range(2)]
        d_y = [dsem(f"d_y{i}") for i in range(2)]

        FXL = [Z0[:, 256 * i:256 * i + 256] for i in range(2)]
        FXT = [Z0[:, 512 + 256 * i:768 + 256 * i] for i in range(2)]
        FS = [Z0[:, 1024 + 512 * i:1536 + 512 * i] for i in range(2)]
        FHT = [Z0[:, 2048 + 512 * i:2560 + 512 * i] for i in range(2)]
        FY = [Z0[:, 3072 + 256 * i:3328 + 256 * i] for i in range(2)]
        FB = [Z0[:, 3584 + 256 * i:3840 + 256 * i] for i in range(2)]

        def experts(layer, nt, xs, ys, w_up, w_down, t_ready, extra, t_eid):
            up_n = 2 * FF if layer == 0 else FF
            t_xl, t_xt, t_xtr, t_up, t_s, t_h, t_ht, t_htr, t_dn, t_y, t_yd, t_w = ({} for _ in range(12))
            regs = {}
            sp.on(t_eid)

            def load_up(i):
                sl = i % 2
                sp.on(t_up.get(2 * (i - 2) + 1))

                def up(e):
                    regs[i] = e.value_load(eidi[0:1, i:i + 1], min_val=0, max_val=E - 1)
                    return e.dma_start(WS[sl][:, 0:2 * up_n].rearrange("p (k n) -> p k n", k=2),
                                       w_up[bass.ds(regs[i] * D, D), :].rearrange("(k p) n -> p k n", p=P))

                t_w[i] = [sp.dma(d_w1[sl], up)]

            def load_down(i):
                sl = i % 2
                sp.on(t_dn.get(2 * (i - 2) + 1))
                t_w[i].append(sp.dma(d_w2[sl], lambda e: e.dma_start(
                    WS[sl][:, 4096:6144].rearrange("p (c n) -> p c n", c=8),
                    w_down[bass.ds(regs[i] * FF, FF), :].rearrange("(c p) n -> p c n", p=P))))
                if layer == 1:
                    sp.on(t_y.get(i - 2), t_ht.get(2 * (i - 2) + 1))
                    sp.dma(d_b[sl], lambda e: e.dma_start(b1c[sl], b11[bass.ds(regs[i] * P, P), :]))
                    t_w[i].append(sp.dma(d_b[sl], lambda e: e.dma_start(
                        FB[sl], b12[bass.ds(regs[i], 1), :].partition_broadcast(P))))

            def load_x(i):
                sp.on(t_xtr.get(i - 2))
                t_xl[i] = load(sp, d_xl[i % 2], FXL[i % 2], xs[i * P:(i + 1) * P, :])

            def turn_x(i):
                def evac(bank, t):
                    ac.on(t, t_up.get(2 * (i - 2) + 1))
                    return ac.do(lambda e: e.activation(FXT[i % 2], bank[:, 0:D], ACT.Copy))

                t_xtr[i], t_xt[i] = turn([FXL[i % 2][:, k * P:k * P + P] for k in range(2)], [t_xl[i]], evac)
                if i + 2 < nt:
                    load_x(i + 2)

            def up(c):
                i, n = divmod(c, 2)
                w = WS[i % 2][:, 0:2 * up_n].rearrange("p (k n) -> p k n", k=2)
                pe.on(t_xt[i], t_w[i][0], t_h.get(c - 2))
                parts = ((0, n * 512), (1, FF + n * 512)) if layer == 0 else ((0, n * 512),)
                for b, o in parts:
                    for k in range(2):
                        t = pe.do(lambda e, b=b, o=o, k=k: e.matmul(
                            PB[2 * (c % 2) + b], FXT[i % 2][:, k * P:k * P + P], w[:, k, o:o + 512],
                            start=k == 0, stop=k == 1), count=k == 1)
                t_up[c] = t
                a, g = PB[2 * (c % 2)], PB[2 * (c % 2) + 1]
                s = FS[c % 2]
                if layer == 0:
                    ac.on(t, t_htr.get(c - 2))
                    t_s[c] = ac.do(lambda e: e.activation(s, a, ACT.Silu))
                    ve.on(t_s[c])
                    t_h[c] = ve.do(lambda e: e.tensor_tensor(s, s, g, ALU.mult))
                else:
                    ve.on(t, t_htr.get(c - 2))
                    t_h[c] = ve.do(lambda e: e.tensor_copy(s, a))

            def turn_h(c):
                i, n = divmod(c, 2)

                def evac(bank, t):
                    ac.on(t, t_dn.get(c - 2))
                    if layer == 0:
                        return ac.do(lambda e: e.activation(FHT[c % 2], bank, ACT.Copy))
                    ac.on(t_w[i][2])
                    for j in range(4):
                        r = ac.do(lambda e, j=j: e.activation(FHT[c % 2][:, j * P:j * P + P], bank[:, j * P:j * P + P],
                                                              ACT.Silu, bias=b1c[i % 2][:, 4 * n + j:4 * n + j + 1]))
                    return r

                t_htr[c], t_ht[c] = turn([FS[c % 2][:, j * P:j * P + P] for j in range(4)], [t_h[c]], evac)

            def down(c):
                i, n = divmod(c, 2)
                w = WS[i % 2][:, 4096:6144].rearrange("p (c n) -> p c n", c=8)
                y = PB[6 + i % 2][:, 0:D]
                pe.on(t_ht[c], t_w[i][1], t_y.get(i - 2))
                for j in range(4):
                    t_dn[c] = pe.do(lambda e, j=j: e.matmul(y, FHT[c % 2][:, j * P:j * P + P], w[:, 4 * n + j, :],
                                                            start=n == 0 and j == 0, stop=n == 1 and j == 3),
                                    count=j == 3)
                if n == 1:
                    ve.on(t_dn[c], t_yd.get(i - 2))
                    if layer == 0:
                        t_y[i] = ve.do(lambda e: e.tensor_copy(FY[i % 2], y))
                    else:
                        ve.on(t_w[i][2])
                        t_y[i] = ve.do(lambda e: e.tensor_tensor(FY[i % 2], y, FB[i % 2], ALU.add))
                    if i + 2 < nt:
                        load_down(i + 2)
                    sp.on(t_y[i])
                    t_yd[i] = load(sp, d_y[i % 2], ys[i * P:(i + 1) * P, :], FY[i % 2])

            sp.on(*t_ready)
            for i in range(2):
                load_x(i)
                load_up(i)
                load_down(i)
            turn_x(0)
            for c in range(2 * nt + 2):
                if c < 2 * nt:
                    up(c)
                    if c % 2 and c // 2 + 2 < nt:
                        load_up(c // 2 + 2)
                if 1 <= c <= 2 * nt:
                    turn_h(c - 1)
                if c % 2 == 0 and c // 2 + 1 < nt:
                    turn_x(c // 2 + 1)
                if c >= 2:
                    down(c - 2)
                extra(c)
            return [t_yd[nt - 2], t_yd[nt - 1]], t_dn[2 * nt - 1]

        def keys_b(c, t_a):
            for f in range(2):
                def evac(bank, t, f=f):
                    ac.on(t)
                    return ac.do(lambda e: e.activation(
                        KS[:, 4 * f:4 * f + 4, c * P:c * P + P], bank.rearrange("p (h k) -> p h k", h=4), ACT.Copy))

                t_kst[c], r = turn([AK[c % 2][:, 4 * f + h, :].bitcast(F32) for h in range(4)], [t_a], evac)
            t_kev.append(r)

        def keys(c):
            if c % 2 == 1 and 1 <= c // 2 + 1 <= NK:
                keys_b(c // 2, keys_a(c // 2))

        t_yd, t_last = experts(0, NT0, xs0, ys0, w01, w02,
                               [*t_scat, t_sct[NC - 1], t_pos, t_x1[NC - 1], t_tr[NC - 1], t_pq], keys, t_eid)

        GR = [Z1[:, 256 * i:256 * i + 256] for i in range(8)]
        d_gr = [dsem(f"d_gr{i}") for i in range(8)]
        t_x2 = {}
        po.on(*t_yd, *t_kst.values())
        po.on((ve.sem, ve.n))
        for c in range(NC):
            po.on(t_x2.get(c - 8))
            t = po.dma(d_gr[c % 8], lambda e, c=c: e.indirect_dma_start(
                GR[c % 8], None, ys0, bass.IndirectOffsetOnAxis(ap=posi[:, c:c + 1].bitcast(U32), axis=0)))
            ve.on(t)
            t_x2[c] = ve.do(lambda e, c=c: e.scalar_tensor_tensor(X[:, c, :], GR[c % 8], pr[:, c:c + 1], X[:, c, :],
                                                                  ALU.mult, ALU.add))
            t = stats(c, t_x2[c])
        inv_std(t)
        t_rq = link(ve, lambda e: e.tensor_scalar(rst2, rst, flag[:, 2:3], None, ALU.mult))

        RW1 = Z0[:, 0:2048].rearrange("p (k n) -> p k n", k=2)
        d_rw = dsem("d_rw")
        sp.on(t_last, (ve.sem, ve.n), (ac.sem, ac.n))
        t_rw = load(sp, d_rw, RW1, rw1.rearrange("(k p) n -> p k n", p=P))
        QT = [Z0[:, 2048 + 128 * i:2176 + 128 * i] for i in range(2)]
        REC, OT = Z0[:, 2304:2816], Z0[:, 2816:3328]
        MP = [Z0[:, 3328 + 16 * i:3344 + 16 * i] for i in range(2)]
        MX, NM = Z0[:, 3360:3364], Z0[:, 3364:3368]
        PT = [Z1[:, 1024 * i:1024 * i + 1024] for i in range(4)]
        t_trf[0], t_trf[1] = t_trf
        PIECE = NK * P // 4
        ring = trn
        t_qs, t_aq, t_qr = {}, {}, {}
        t_qfree = {}
        t_at = {}
        t_aut = {}
        qn = [0]

        def maxima(n):
            qg, hf = divmod(n, 2)
            q = QS[n % 2]
            for t4 in range(4):
                c = 4 * qg + t4
                j = qn[0]
                qn[0] += 1
                a = AK[j % 2]
                qt = QT[j % 2]
                q3 = qt.rearrange("p (h d) -> p h d", h=4)
                ve.on(t_aq.get(j - 2), *t_kst.values())
                t = ve.do(lambda e, c=c, qt=qt: e.tensor_scalar(
                    qt, X[:, c, hf * P:hf * P + P], mean[:, c:c + 1], rst2[:, c:c + 1], ALU.subtract, ALU.mult))
                ve.on(t)
                t = ve.do(lambda e, a=a, q3=q3: e.tensor_copy(a[:, 0:4, 0:32], q3))
                ve.do(lambda e, a=a, q3=q3: e.tensor_copy(a[:, 0:4, 64:96], q3))
                if j < 2:
                    ve.do(lambda e, a=a: e.memset(a[:, 0:4, 97:98].bitcast(F32), 0.0))
                    ve.do(lambda e, a=a: e.memset(a[:, 0:4, 99:100].bitcast(F32), 0.0))
                    ve.do(lambda e, a=a: e.memset(a[:, 0:4, 96:97].bitcast(F32), 1.0))
                    ve.do(lambda e, a=a: e.memset(a[:, 0:4, 98:99].bitcast(F32), 1.0))
                ve.on(t)
                t = ve.do(lambda e, a=a, q3=q3: e.tensor_tensor(a[:, 0:4, 32:64], q3, a[:, 0:4, 0:32].bitcast(F32),
                                                                ALU.subtract))

                def evac(bank, tt_, t4=t4):
                    ve.on(tt_, t_qfree.get(n - 2))
                    return ve.do(lambda e: e.tensor_copy(q[:, :, t4 * P:t4 * P + P],
                                                         bank.rearrange("p (h k) -> p h k", h=4)))

                t_aq[j], t_q = turn([a[:, h, :].bitcast(F32) for h in range(4)], [t], evac)
                yield
                mp = MP[j % 2]
                for h in range(4):
                    for s in range(4):
                        b = ring[0] % 2
                        ring[0] += 1
                        pe.on(t_q, t_trf[b])
                        t = pe.do(lambda e, h=h, s=s, b=b, t4=t4: e.matmul(
                            PB[4 + b][:, 0:PIECE], q[:, h, t4 * P:t4 * P + P],
                            KS[:, 4 * hf + h, s * PIECE:(s + 1) * PIECE], start=True, stop=True))
                        ve.on(t)
                        t_trf[b] = ve.do(lambda e, h=h, s=s, b=b, mp=mp: e.tensor_reduce(
                            mp[:, 4 * h + s:4 * h + s + 1], PB[4 + b][:, 0:PIECE], AX.X, ALU.max))
                        yield
                au = AU[j % 2]
                ve.on(t_trf[(ring[0] - 1) % 2], t_aut.get(j - 2), t_au)
                link(ve, lambda e, mp=mp: e.tensor_reduce(MX, mp.rearrange("p (h s) -> p h s", s=4), AX.X, ALU.max))
                link(ve, lambda e: e.tensor_scalar(NM, MX, -1.0, None, ALU.mult))
                t = ve.do(lambda e, au=au: e.tensor_copy(au[:, :, 97:98], NM.unsqueeze(2)))
                ve.on(t)
                t = ve.do(lambda e, au=au: e.tensor_tensor(au[:, :, 99:100], NM.unsqueeze(2),
                                                           au[:, :, 97:98].bitcast(F32), ALU.subtract))

                def evac2(bank, tt_, t4=t4):
                    ve.on(tt_)
                    return ve.do(lambda e: e.tensor_copy(
                        q[96:128, :, t4 * P:t4 * P + P], bank[96:128, :].rearrange("p (h k) -> p h k", h=4)))

                t_aut[j], t_qs[n] = turn([au[:, h, :].bitcast(F32) for h in range(4)], [t], evac2)
                yield

        t_bank = [None, None]
        t_pt = {}
        pairs = [0]
        t_x3 = {}

        def attend(n, side):
            qg, hf = divmod(n, 2)
            q = QS[n % 2]
            exps = {}

            def scores(kc):
                for pr_ in range(2):
                    pe.on(t_qs[n], *t_kev, t_bank[pr_])
                    for h in range(2):
                        hh = 2 * pr_ + h
                        t = pe.do(lambda e, pr_=pr_, h=h, hh=hh: e.matmul(
                            PB[2 * pr_ + h], KS[:, 4 * hf + hh, kc * P:kc * P + P], q[:, hh, :],
                            start=True, stop=True), count=h == 1)
                    g = pairs[0]
                    pairs[0] += 1
                    ac.on(t, t_pt.get(g - 4), t_x2[NC - 1])
                    t_bank[pr_] = ac.do(lambda e, g=g, pr_=pr_: e.activation(
                        PT[g % 4], PQ[:, 1024 * pr_:1024 * pr_ + 1024], ACT.Exp))
                    exps[(kc, pr_)] = (g, t_bank[pr_])
                if kc == NK - 1:
                    t_qfree[n] = t

            def values(kc):
                for pr_ in range(2):
                    g, t = exps[(kc, pr_)]
                    pe.on(t)
                    if kc == 0:
                        pe.on(t_at.get(n - 1), t_last, t_yd[1], (0 and None) or t_x3.get("o"))
                    for h in range(2):
                        hh = 2 * pr_ + h
                        for bank, lhs in ((6, V[:, kc, (4 * hf + hh) * 32:(4 * hf + hh) * 32 + 32]), (7, ones[:, 0:32])):
                            t_pt[g] = pe.do(lambda e, bank=bank, lhs=lhs, hh=hh, g=g, h=h: e.matmul(
                                PB[bank][32 * hh:32 * hh + 32, :], lhs, PT[g % 4][:, 512 * h:512 * h + 512],
                                start=kc == 0, stop=kc == NK - 1, tile_position=(0, 32 * hh)), count=h == 1 and bank == 7)

            for kc in range(NK + 1):
                if kc < NK:
                    scores(kc)
                for _ in range(3):
                    next(side, None)
                if kc >= 1:
                    values(kc - 1)
                for _ in range(3):
                    next(side, None)
            for _ in side:
                pass
            ve.on(t_pt[pairs[0] - 1])
            t = ve.do(lambda e: e.reciprocal(REC, PB[7]))
            ve.on(t, t_x3.get("t"))
            t = ve.do(lambda e: e.tensor_tensor(OT, PB[6], REC, ALU.mult))
            t_at[n] = t

            def evac(bank, tt_):
                ve.on(tt_)
                v = X[:, 4 * qg:4 * qg + 4, hf * P:hf * P + P]
                return ve.do(lambda e: e.scalar_tensor_tensor(v, bank.rearrange("p (c d) -> p c d", c=4), tg[:, 1:2], v,
                                                              ALU.mult, ALU.add))

            t_x3["t"], t_x3[n] = turn([OT[:, j * P:j * P + P] for j in range(4)], [t], evac)

        pe.on(*t_yd)
        for _ in maxima(0):
            pass
        for n in range(8):
            attend(n, maxima(n + 1) if n < 7 else iter(()))

        for c in range(NC):
            t = stats(c, t_x3[7])
        inv_std(t)
        XR = [Z1[:, 256 * i:256 * i + 256] for i in range(4)]
        XG = [Z1[:, 1024 + 1024 * i:2048 + 1024 * i].rearrange("p (k q) -> p k q", k=2) for i in range(2)]
        HR = [Z1[:, 3072 + 512 * i:3584 + 512 * i] for i in range(2)]
        LT = Z0[0:8, 2048:2560]
        t_xn, t_xtr, t_xg, t_hb, t_hr, t_lm, t_rb = {}, {}, {}, {}, {}, {}, {}
        ve.on(t_pt[pairs[0] - 1])
        t_lt = None
        for g in range(4):
            for t4 in range(4):
                c = 4 * g + t4
                ve.on(t_xtr.get(c - 4))
                t_xn[c] = ve.do(lambda e, c=c: e.tensor_scalar(XR[c % 4], X[:, c, :], mean[:, c:c + 1],
                                                               rst[:, c:c + 1], ALU.subtract, ALU.mult))

                def evac(bank, t, g=g, t4=t4):
                    ve.on(t, t_rb.get(8 * (g - 2) + 7))
                    return ve.do(lambda e: e.tensor_copy(XG[g % 2][:, :, t4 * P:t4 * P + P],
                                                         bank[:, 0:D].rearrange("p (k q) -> p k q", k=2)))

                t_xtr[c], t_xg[g] = turn([XR[c % 4][:, k * P:k * P + P] for k in range(2)], [t_xn[c]], evac)
            for f in range(9):
                if f < 8:
                    m = 8 * g + f
                    pe.on(t_xg[g], t_rw, t_hr.get(m - 4), t_bank[0], t_bank[1])
                    for k in range(2):
                        t_rb[m] = pe.do(lambda e, k=k, m=m, f=f, g=g: e.matmul(
                            PB[m % 4], RW1[:, k, f * P:f * P + P], XG[g % 2][:, k, :], start=k == 0, stop=k == 1))
                    ac.on(t_rb[m], t_lm.get(m - 2))
                    t_hr[m] = ac.do(lambda e, m=m, f=f: e.activation(HR[m % 2], PB[m % 4], ACT.Silu,
                                                                     bias=rb1s[:, f:f + 1]))
                if f >= 1:
                    m = 8 * g + f - 1
                    pe.on(t_hr[m], t_lt, t_at[7])
                    t_lm[m] = pe.do(lambda e, m=m, f=f: e.matmul(PB[6][0:8, :], rw2s[:, 8 * f - 8:8 * f], HR[m % 2],
                                                                 start=f == 1, stop=f == 8))
            ve.on(t_lm[8 * g + 7], t_x3.get(("l", g - 1)), t_at[7])
            t_lt = ve.do(lambda e: e.tensor_copy(LT, PB[6][0:8, :]))
            pe.on(t_lt)
            for t4 in range(4):
                c = 4 * g + t4
                t_x3[("l", g)] = pe.do(lambda e, c=c, t4=t4: e.transpose(PB[7][:, c * E:c * E + E],
                                                                         LT[:, t4 * P:t4 * P + P], ident[0:8, 0:8]))
        pe.on(t_trf[0], t_trf[1])
        t_pos, t_eid = route(2, PB[7][:, 0:NC * E].rearrange("p (c e) -> p c e", e=E), rb2s, NT1, t_x3[("l", 3)])

        t_sct = {}
        po.on(t_pos)
        ve.on(t_xtr[NC - 1])
        for c in range(NC):
            ve.on(t_sct.get(c - 4))
            t = ve.do(lambda e, c=c: e.tensor_scalar(XR[c % 4], X[:, c, :], mean[:, c:c + 1],
                                                     rst[:, c:c + 1], ALU.subtract, ALU.mult))
            t_sct[c] = scatter(c, XR[c % 4], xs1, t, 2, d_sc[c % 4], None)
        t_scat = [t_sct[c] for c in range(NC - 4, NC)]

        t_yd, t_last = experts(1, NT1, xs1, ys1, w11, w12, [*t_scat, t_rb[31], (ac.sem, ac.n), (ve.sem, ve.n)],
                               lambda c: None, t_eid)
        po.on(*t_yd)
        t_o = {}
        d_o = dsem("d_o")
        t_free = {}
        for c in range(NC):
            g1, g2 = GR[(2 * c) % 8], GR[(2 * c + 1) % 8]
            for k, g in ((0, g1), (1, g2)):
                po.on(t_free.get(c - 4))
                t = po.dma(d_gr[(2 * c + k) % 8], lambda e, c=c, k=k, g=g: e.indirect_dma_start(
                    g, None, ys1, bass.IndirectOffsetOnAxis(ap=posi[:, k * NC + c:k * NC + c + 1].bitcast(U32), axis=0)))
                ve.on(t)
                t = ve.do(lambda e, c=c, k=k, g=g: e.scalar_tensor_tensor(X[:, c, :], g, pr[:, k * NC + c:k * NC + c + 1],
                                                                         X[:, c, :], ALU.mult, ALU.add))
                ve.on(t)
            t_free[c] = t
            sp.on(t)
            load(sp, d_o, out[c * P:(c + 1) * P, :], X[:, c, :])
        sp.on((d_o.sem, d_o.n))

        block = es.enter_context(nc.Block())

        @block.sync
        def _(e):
            sp.play(e)

        @block.tensor
        def _(e):
            pe.play(e)

        @block.scalar
        def _(e):
            ac.play(e)

        @block.vector
        def _(e):
            ve.play(e)

        @block.gpsimd
        def _(e):
            po.play(e)


def kernel(x, ctx_2048, mask_BxS2_if0, mask_BxS2_ik0, g_xattn, g_ffn, L0_xattn_W_in, L0_xattn_b_in, L0_xattn_g_res,
           L0_xattn_g_init, L0_ffn_router_w, L0_ffn_router_b, L0_ffn_w1, L0_ffn_w2, L1_xattn_b, L1_ffn_rw1,
           L1_ffn_rb1, L1_ffn_rw2, L1_ffn_rb2, L1_ffn_w1, L1_ffn_b1, L1_ffn_w2, L1_ffn_b2):
    import concourse.bacc as bacc
    from concourse.bass_utils import run_bass_kernel_spmd

    def arr(a, *shape):
        return np.ascontiguousarray(np.asarray(a).reshape(shape))

    def by_partition(a, n):
        a = np.asarray(a).reshape(-1)
        r = np.zeros(n * P, a.dtype)
        r[:a.size] = a
        return np.ascontiguousarray(r.reshape(n, P).T)

    ins = {
        "cst": constants(),
        "x": arr(x, T, D),
        "ctx_2048": arr(ctx_2048, S2, 2 * D),
        "plen": arr(mask_BxS2_if0, 1, S2),
        "kmask": by_partition(mask_BxS2_ik0, NK),
        "g_xattn": arr(g_xattn, 1, 2),
        "g_ffn": arr(g_ffn, 1, 2),
        "W_in": np.ascontiguousarray(np.asarray(L0_xattn_W_in).T),
        "b_in": arr(L0_xattn_b_in, 1, D),
        "g_res": by_partition(L0_xattn_g_res, 2),
        "g_init": arr(L0_xattn_g_init, 1, 2 * D),
        "rw0": arr(L0_ffn_router_w, D, E),
        "rb0": arr(L0_ffn_router_b, 1, E),
        "w01": arr(L0_ffn_w1, E * D, 2 * FF),
        "w02": arr(L0_ffn_w2, E * FF, D),
        "att_b": arr(L1_xattn_b, 1, 1),
        "rw1": arr(L1_ffn_rw1, D, FF),
        "rb1": by_partition(L1_ffn_rb1, 8),
        "rw2": arr(L1_ffn_rw2, FF, E),
        "rb2": arr(L1_ffn_rb2, 1, E),
        "w11": arr(L1_ffn_w1, E * D, FF),
        "b11": np.ascontiguousarray(np.asarray(L1_ffn_b1).reshape(E, 8, P).transpose(0, 2, 1).reshape(E * P, 8)),
        "w12": arr(L1_ffn_w2, E * FF, D),
        "b12": arr(L1_ffn_b2, E, D),
    }
    nc = bacc.Bacc("TRN2", target_bir_lowering=False, num_devices=1)
    args, arrays = {}, {}
    for name, a in ins.items():
        arrays["in_" + name] = a
        args[name] = nc.dram_tensor("in_" + name, a.shape, mybir.dt.from_np(a.dtype), kind="ExternalInput").ap()
    out = nc.dram_tensor("out_0", (T, D), F32, kind="ExternalOutput").ap()
    build(nc, out=out, **args)
    r = run_bass_kernel_spmd(nc, [arrays], core_ids=[0])
    return np.asarray(r.results[0]["out_0"]).reshape(1, T, D)
```

```python
from contextlib import ExitStack

import numpy as np
import concourse.bass as bass
from concourse import mybir

F32 = mybir.dt.float32
F32R = mybir.dt.float32r
I32 = mybir.dt.int32
U32 = mybir.dt.uint32
ALU = mybir.AluOpType
ACT = mybir.ActivationFunctionType
AX = mybir.AxisListType

P = 128
D = 256
T = 2048
NC = T // P
S2 = 1601
NK = 13
REM = S2 - 12 * P
E = 8
FF = 1024
NT0 = T // P + E - 1
NT1 = 2 * T // P + E - 1
EPS = 1e-5
MASKED = -1e30
BEYOND = -3e38

C_ID, C_L, C_L2, C_U, C_ONE = 0, 128, 256, 384, 512
C_SEG, C_IO8, C_IOT, C_TP, C_SEG16 = 640, 896, 904, 944, 960
C_PAD, C_LAST, C_UI, C_I128 = 1088, 1089, 1090, 1218
C_N = 1346
SMN = 2960


def constants():
    c = np.zeros((P, C_N), np.float32)
    dt = -np.log(-np.expm1(-0.001))
    a = np.exp(-dt)
    j = np.arange(P)
    gap = (j[None, :] - j[:, None]).astype(np.float64)
    c[:, C_ID:C_ID + P] = np.eye(P)
    c[:, C_L:C_L + P] = np.where(gap >= 0, np.power(a, np.maximum(gap, 0)), 0.0)
    c[:, C_L2:C_L2 + P] = np.power(a, np.minimum(gap + P, 60.0))
    c[:, C_U:C_U + P] = gap > 0
    c[:, C_ONE:C_ONE + P] = 1.0
    seg = np.ones((E, 32), np.float32)
    seg[:, 0] = 0.0
    c[:, C_SEG:C_SEG + E * 32] = seg.reshape(-1)
    c[:, C_SEG16:C_SEG16 + E * 16] = seg[:, :16].reshape(-1)
    c[:, C_IO8:C_IO8 + E] = np.arange(E)
    c[:, C_IOT:C_IOT + 40] = np.arange(40)
    c[:, C_TP:C_TP + NC] = np.arange(NC)[None, :] * P + j[:, None] + 1
    c[REM:, C_PAD] = BEYOND
    c[P - 1, C_LAST] = 1.0
    c[:, C_UI:C_UI + P] = gap >= 0
    c[:, C_I128:C_I128 + P] = j[None, :]
    return c


class Queue:

    def __init__(self, sem):
        self.sem, self.n, self.ops, self.seen = sem, 0, [], {}

    def do(self, make, count=True):
        if count:
            self.n += 1
            self.ops.append(lambda e: make(e).then_inc(self.sem, 1))
            return (self.sem, self.n)
        self.ops.append(make)
        return None

    def on(self, *tokens):
        for token in tokens:
            if token is None:
                continue
            sem, n = token
            if self.seen.get(sem.name, 0) < n:
                self.seen[sem.name] = n
                self.ops.append(lambda e, sem=sem, n=n: e.wait_ge(sem, n))

    def dma(self, dsem, make):
        dsem.n += 16
        self.ops.append(lambda e: make(e).then_inc(dsem.sem, 16))
        return (dsem.sem, dsem.n)

    def play(self, e):
        for op in self.ops:
            op(e)


class DmaSem:
    def __init__(self, sem):
        self.sem, self.n = sem, 0


def build(nc, cst, x, ctx_2048, plen, kmask, g_xattn, g_ffn, W_in, b_in, g_res, g_init, rw0, rb0, w01, w02,
          att_b, rw1, rb1, rw2, rb2, w11, b11, w12, b12, out):
    es = ExitStack()
    with es:
        def sb(name, shape, dt=F32):
            return es.enter_context(nc.sbuf_tensor(name, shape, dt))[:, :]

        def queue(name):
            return Queue(es.enter_context(nc.semaphore(name)))

        def dsem(name):
            return DmaSem(es.enter_context(nc.semaphore(name)))

        sp, pe, ac, ve, po = (queue(n) for n in ("q_sp", "q_pe", "q_ac", "q_ve", "q_po"))

        X = sb("X", [P, NC * D]).rearrange("p (c d) -> p c d", d=D)
        WS = [sb(f"WS{i}", [P, 6144]) for i in range(2)]
        KS = sb("KS", [P, E * NK * P], F32R).rearrange("p (h k) -> p h k", h=E)
        V = sb("V", [P, NK * D]).rearrange("p (c d) -> p c d", d=D)
        Z0 = sb("Z0", [P, 4096])
        Z1 = sb("Z1", [P, 4096])
        QS = [sb(f"QS{i}", [P, 2048], F32R).rearrange("p (h q) -> p h q", h=4) for i in range(2)]
        AK = [sb(f"AK{i}", [P, 1024], F32R).rearrange("p (h c) -> p h c", h=8) for i in range(2)]
        AU = [sb(f"AU{i}", [P, 512], F32R).rearrange("p (h c) -> p h c", h=4) for i in range(2)]
        MBH = sb("MBH", [P, 2 * NK], F32R)
        CT = sb("CT", [P, C_N])
        SM = sb("SM", [P, SMN])
        SI = sb("SI", [P, 128], I32)
        CK = Z1[:, 0:NK * D].rearrange("p (c d) -> p c d", d=D)
        PQ = es.enter_context(nc.psum_tensor("PQ", [P, 2048], F32))[:, :]
        PB = [PQ[:, 512 * i:512 * i + 512] for i in range(4)]
        PB += [es.enter_context(nc.psum_tensor(f"PB{i}", [P, 512], F32))[:, :] for i in range(4, 8)]

        def scratch(name, rows):
            return nc.dram_tensor(name, [rows, D], F32, kind="Internal").ap()

        dep_d, xs0, ys0, xs1, ys1 = (scratch(n, r) for n, r in (
            ("dep_d", NK * P), ("xs0", NT0 * P), ("ys0", NT0 * P), ("xs1", NT1 * P), ("ys1", NT1 * P)))

        at = [0]

        def sm(n):
            at[0] += n
            assert at[0] <= SMN, at[0]
            return SM[:, at[0] - n:at[0]]

        ident, ones = CT[:, C_ID:C_ID + P], CT[:, C_ONE:C_ONE + P]
        gates, tg, attb, gres = sm(4), sm(4), sm(1), sm(2)
        rw0s, rb0s, rb1s, rw2s, rb2s = sm(16), sm(8), sm(8), sm(64), sm(8)
        ssk, ssv, rs, mb = sm(NK), sm(NK), sm(NK), sm(NK)
        st6, mv, rst, rst2, nh = sm(NC * 6), sm(NC * 2), sm(NC), sm(NC), sm(16)
        flag = sm(4)
        lg, la, OH = sm(NC * E), sm(NC * E), sm(2 * NC * E)
        inc, rk = sm(2 * NC * E), sm(2 * NC * E)
        m1, m2, pr, tt, pos = sm(NC), sm(NC), sm(2 * NC), sm(NC), sm(2 * NC)
        cnt, nti, bi, bas = sm(E), sm(E), sm(E), sm(E)
        b1c = [sm(8), sm(8)]
        mxx, sc7 = sm(80), sm(280)
        plugi, posi, eidi, ntii, mski = SI[:, 0:16], SI[:, 16:48], SI[:, 48:88], SI[:, 88:96], SI[:, 96:109]

        d_c, d_s, d_p, d_k, d_v, d_x = (dsem(n) for n in ("d_c", "d_s", "d_p", "d_k", "d_v", "d_x"))
        Win = Z0[:, 0:512].rearrange("p (k n) -> p k n", k=2)
        gIB, bIB = Z0[:, 512:768], Z0[:, 768:1024]
        U3 = [Z0[:, 1024 + 256 * i:1280 + 256 * i] for i in range(3)]
        DR = [Z0[:, 1792 + 256 * i:2048 + 256 * i] for i in range(2)]
        def load(q, d, dst, src):
            return q.dma(d, lambda e: e.dma_start(dst, src))

        t_p = load(sp, d_p, SI[:, 109:122], plen)
        for c in range(0, NC, 4):
            t_x = load(sp, d_x, X[:, c:c + 4, :], x[c * P:(c + 4) * P, :].rearrange("(c p) d -> p c d", p=P))
        t_mz = ve.do(lambda e: e.memset(CK[:, 12, :], 0.0))
        t_vz = ve.do(lambda e: e.memset(V[:, 12, :], 0.0))
        load(ac, d_c, CT, cst)
        t_c = (d_c.sem, 16)
        load(ac, d_k, CK[:, 0:12, :], ctx_2048[0:12 * P, 0:D].rearrange("(c p) d -> p c d", p=P))
        ac.on(t_mz, t_vz)
        load(ac, d_k, CK[0:REM, 12, :], ctx_2048[12 * P:S2, 0:D])
        load(ac, d_k, V[:, 0:12, :], ctx_2048[0:12 * P, D:2 * D].rearrange("(c p) d -> p c d", p=P))
        load(ac, d_k, V[0:REM, 12, :], ctx_2048[12 * P:S2, D:2 * D])
        t_k = load(ac, d_k, mski, kmask)
        load(sp, d_s, gIB, g_init[:, 0:D].partition_broadcast(P))
        load(sp, d_s, bIB, b_in.partition_broadcast(P))
        load(sp, d_s, Win, W_in.rearrange("(k p) n -> p k n", p=P))
        load(sp, d_s, gres, g_res)
        load(sp, d_s, gates[:, 0:2], g_xattn.partition_broadcast(P))
        load(sp, d_s, gates[:, 2:4], g_ffn.partition_broadcast(P))
        load(sp, d_s, attb, att_b.partition_broadcast(P))
        load(sp, d_s, rw0s.rearrange("p (k n) -> p k n", k=2), rw0.rearrange("(k p) n -> p k n", p=P))
        load(sp, d_s, rb0s, rb0.partition_broadcast(P))
        load(sp, d_s, rb1s, rb1)
        load(sp, d_s, rw2s.rearrange("p (k n) -> p k n", k=8), rw2.rearrange("(k p) n -> p k n", p=P))
        t_s = load(sp, d_s, rb2s, rb2.partition_broadcast(P))

        zero = WS[1][:, 3072:5120]
        t_z = po.do(lambda e: e.memset(zero, 0.0))
        po.do(lambda e: e.memset(nh, -0.5))
        d_z = [dsem("d_z0"), dsem("d_z1")]

        def clear(i, buf, nt):
            v = buf.rearrange("(p r) d -> p (r d)", p=P)
            for r in range(0, nt, 8):
                k = min(8, nt - r)
                t = load(ac, d_z[i], v[:, r * D:(r + k) * D], zero[:, 0:k * D])
            return t

        for t in AK + AU:
            po.do(lambda e, t=t: e.memset(t[:, :, 96:128].bitcast(F32), 0.0))
        for t in AU:
            po.do(lambda e, t=t: e.memset(t[:, :, 0:96].bitcast(F32), 0.0))
        po.on((po.sem, po.n))
        for t in AU:
            po.do(lambda e, t=t: e.memset(t[:, :, 96:97].bitcast(F32), 1.0))
            t_au = po.do(lambda e, t=t: e.memset(t[:, :, 98:99].bitcast(F32), 1.0))
        for t in AK:
            po.do(lambda e, t=t: e.memset(t[:, :, 97:98].bitcast(F32), 1.0))
            t_au = po.do(lambda e, t=t: e.memset(t[:, :, 99:100].bitcast(F32), 1.0))

        ac.on(t_s, t_z)
        t_zero = clear(0, xs0, NT0)
        t_zero1 = clear(1, xs1, NT1)
        t_tg = ac.do(lambda e: e.activation(tg, gates, ACT.Tanh))

        def link(q, make):
            t = q.do(make)
            q.on(t)
            return t

        lenf, vv, hi, lo = sm(NK), sm(NK), sm(NK), sm(NK)
        hst, cn, wrp = sm(NC), sm(NC), sm(4)
        hoh = sm(NK * NC).rearrange("p (j c) -> p j c", c=NC)
        LOH = Z0[:, 2304:2304 + NK * P].rearrange("p (j q) -> p j q", q=P)
        leni, poi = SI[:, 109:122], SI[:, 56:69]
        iota128 = CT[:, C_I128:C_I128 + P]
        ve.on(t_p, t_c)
        link(ve, lambda e: e.tensor_scalar(lenf, leni, 4096.0, None, ALU.min))
        pe.on((ve.sem, ve.n), t_c)
        pe.do(lambda e: e.matmul(PB[0][:, 0:NK], CT[:, C_UI:C_UI + P], lenf, start=True, stop=True))
        pe.do(lambda e: e.matmul(PB[1][:, 0:NK], ones, lenf, start=True, stop=True))
        t = pe.do(lambda e: e.matmul(PB[2][:, 0:1], ones[0:1, :], lenf[0:1, 0:1], start=True, stop=True))
        ve.on(t)
        link(ve, lambda e: e.tensor_tensor_scan(hi, ones[:, 0:NK], PB[1][:, 0:NK], 0.0, ALU.mult, ALU.add))
        link(ve, lambda e: e.tensor_tensor(hi, hi, PB[1][:, 0:NK], ALU.subtract))
        link(ve, lambda e: e.tensor_tensor(vv, hi, PB[0][:, 0:NK], ALU.add))
        link(ve, lambda e: e.tensor_single_scalar(hi, lenf, 0.0, ALU.is_equal))
        link(ve, lambda e: e.scalar_tensor_tensor(vv, hi, 4.0e6, vv, ALU.mult, ALU.add))
        link(ve, lambda e: e.tensor_scalar(poi, vv, -1.0, None, ALU.add))
        poh = SI[:, 69:82]
        link(ve, lambda e: e.tensor_single_scalar(poh, poi, 7, ALU.arith_shift_right))
        link(ve, lambda e: e.tensor_copy(hi, poh))
        link(ve, lambda e: e.scalar_tensor_tensor(lo, hi, -float(P), vv, ALU.mult, ALU.add))
        link(ve, lambda e: e.tensor_scalar(lo, lo, -1.0, None, ALU.add))
        ve.do(lambda e: e.tensor_tensor(hoh, hi.unsqueeze(2).broadcast_to([P, NK, NC]),
                                        iota128[:, 0:NC].unsqueeze(1).broadcast_to([P, NK, NC]), ALU.is_equal))
        link(ve, lambda e: e.tensor_tensor(LOH, lo.unsqueeze(2).broadcast_to([P, NK, P]),
                                           iota128.unsqueeze(1).broadcast_to([P, NK, P]), ALU.is_equal))
        pe.on((ve.sem, ve.n))
        for j in range(NK):
            t = pe.do(lambda e, j=j: e.matmul(PB[3][:, 0:NC], LOH[:, j, :], hoh[:, j, :], start=j == 0,
                                              stop=j == NK - 1), count=j == NK - 1)
        ve.on(t)
        link(ve, lambda e: e.tensor_copy(hst, PB[3][:, 0:NC]))
        pe.on((ve.sem, ve.n))
        pe.do(lambda e: e.matmul(PB[0][:, 0:NC], CT[:, C_UI:C_UI + P], hst, start=True, stop=True))
        t = pe.do(lambda e: e.matmul(PB[1][:, 0:NC], ones, hst, start=True, stop=True))
        ve.on(t)
        link(ve, lambda e: e.tensor_tensor_scan(cn, ones[:, 0:NC], PB[1][:, 0:NC], 0.0, ALU.mult, ALU.add))
        link(ve, lambda e: e.tensor_tensor(cn, cn, PB[1][:, 0:NC], ALU.subtract))
        link(ve, lambda e: e.tensor_tensor(cn, cn, PB[0][:, 0:NC], ALU.add))
        link(ve, lambda e: e.tensor_single_scalar(wrp[:, 0:1], PB[2][:, 0:1], 0.0, ALU.is_equal))
        link(ve, lambda e: e.tensor_single_scalar(wrp[:, 1:2], hst[:, 15:16], 0.0, ALU.is_equal))
        link(ve, lambda e: e.tensor_tensor(wrp[:, 2:3], wrp[:, 0:1], wrp[:, 1:2], ALU.mult))
        link(ve, lambda e: e.scalar_tensor_tensor(cn[:, 15:16], CT[:, C_LAST:C_LAST + 1], wrp[:, 2:3], cn[:, 15:16],
                                                  ALU.mult, ALU.add))
        t_pq = (ve.sem, ve.n)
        link(ve, lambda e: e.tensor_scalar(tt, cn, 1.0, float(S2 - 1), ALU.subtract, ALU.min))
        link(ve, lambda e: e.tensor_scalar(tt, tt, 0.0, None, ALU.max))
        t_plug = link(ve, lambda e: e.tensor_copy(plugi, tt))

        ve.on(t_k)
        ac.on(t_k, t_mz, t_vz)
        for c in range(NK):
            ac.do(lambda e, c=c: e.activation(PB[4][:, 0:D], CK[:, c, :], ACT.Square, accum_out=ssk[:, c:c + 1]))
            t_ss = ac.do(lambda e, c=c: e.activation(PB[5][:, 0:D], V[:, c, :], ACT.Square, accum_out=ssv[:, c:c + 1]))
            ac.on(t_ss)
        ve.on(t_ss)
        link(ve, lambda e: e.tensor_tensor(rs, ssk, ssv, ALU.add))
        t = link(ve, lambda e: e.tensor_scalar(rs, rs, 1.0 / (2 * D), EPS, ALU.mult, ALU.add))
        po.on(t)
        t = link(po, lambda e: e.tensor_tensor(rs, rs, nh[:, 0:NK], ALU.pow))
        ve.on(t)
        link(ve, lambda e: e.tensor_scalar(rs, rs, float(np.float32(np.exp(-0.001))), None, ALU.mult))

        d_dr = [dsem(f"d_dr{i}") for i in range(2)]
        t_u, t_sc, t_dr = [], [], []
        def evac_dep(c):
            ve.on(t_sc[c])
            if c >= 2:
                ve.on(t_dr[c - 2])
            t = ve.do(lambda e: e.tensor_tensor(DR[c % 2], PB[6 + c % 2][:, 0:D], bIB, ALU.add))
            sp.on(t)
            t_dr.append(load(sp, d_dr[c % 2], dep_d[c * P:(c + 1) * P, :], DR[c % 2]))
            return t

        for c in range(NK):
            if c >= 3:
                ve.on(t_sc[c - 2])
            t_u.append(ve.do(lambda e, c=c: e.scalar_tensor_tensor(U3[c % 3], CK[:, c, :], rs[:, c:c + 1], gIB,
                                                                   ALU.mult, ALU.mult)))
            bank = PB[6 + c % 2][:, 0:D]
            pe.on(t_u[c])
            if c >= 2:
                pe.on(t_ev)
            pe.do(lambda e, c=c, bank=bank: e.matmul(bank, CT[:, C_L:C_L + P], U3[c % 3], start=True, stop=c == 0),
                  count=c == 0)
            if c:
                pe.do(lambda e, c=c, bank=bank: e.matmul(bank, CT[:, C_L2:C_L2 + P], U3[(c - 1) % 3],
                                                         start=False, stop=True))
            t_sc.append((pe.sem, pe.n))
            if c >= 1:
                t_ev = evac_dep(c - 1)
        t_ev = evac_dep(NK - 1)

        def stats(c, after=None):
            ve.on(after)
            t = ve.do(lambda e: e.bn_stats(st6[:, 6 * c:6 * c + 6], X[:, c, :]))
            ve.on(t)
            return ve.do(lambda e: e.bn_aggr(mv[:, 2 * c:2 * c + 2], st6[:, 6 * c:6 * c + 6]))

        mean = mv.rearrange("p (c s) -> p c s", s=2)[:, :, 0]
        var = mv.rearrange("p (c s) -> p c s", s=2)[:, :, 1]

        def inv_std(after, a=0, b=NC):
            ve.on(after)
            t = ve.do(lambda e: e.tensor_scalar(rst[:, a:b], var[:, a:b], EPS, None, ALU.add))
            po.on(t)
            return po.do(lambda e: e.tensor_tensor(rst[:, a:b], rst[:, a:b], nh[:, a:b], ALU.pow))

        ve.on((d_x.sem, 64))
        for c in range(NC):
            t = stats(c)
        ve.on(inv_std(t))
        link(ve, lambda e: e.tensor_tensor(rst2, rst, rst, ALU.mult))
        link(ve, lambda e: e.tensor_tensor(rst2, rst2, var, ALU.mult))
        t = link(ve, lambda e: e.tensor_scalar(rst2, rst2, EPS, None, ALU.add))
        po.on(t)
        t = link(po, lambda e: e.tensor_tensor(rst2, rst2, nh, ALU.pow))
        ve.on(t)
        link(ve, lambda e: e.tensor_tensor(rst2, rst2, rst, ALU.mult))
        for k in range(2):
            t_win = ve.do(lambda e, k=k: e.tensor_scalar(Win[:, k, :], Win[:, k, :], gres[:, k:k + 1], None, ALU.mult))

        HIN = [WS[1][:, 256 * i:256 * i + 256] for i in range(4)]
        HT = [WS[1][:, 1024 + 256 * i:1280 + 256 * i] for i in range(4)]
        DG = [WS[1][:, 2048 + 256 * i:2304 + 256 * i] for i in range(4)]
        d_dg = [dsem(f"d_dg{i}") for i in range(4)]
        t_hin, t_tr, t_ht, t_mm, t_dg, t_x1, t_st = {}, {}, {}, {}, {}, {}, {}

        po.on(t_plug, *t_dr[-2:])
        for c in range(NC + 2):
            if c < NC:
                if c >= 4:
                    po.on(t_x1[c - 4])
                t_dg[c] = po.dma(d_dg[c % 4], lambda e, c=c: e.indirect_dma_start(
                    DG[c % 4], None, dep_d, bass.IndirectOffsetOnAxis(ap=plugi[:, c:c + 1].bitcast(U32), axis=0)))
                if c >= 4:
                    ve.on(t_tr[c - 4])
                t_hin[c] = ve.do(lambda e, c=c: e.tensor_scalar(HIN[c % 4], X[:, c, :], mean[:, c:c + 1],
                                                                rst2[:, c:c + 1], ALU.subtract, ALU.mult))
                pe.on(t_hin[c], t_pq, t_ss, t_ht.get(c - 2))
                for k in range(2):
                    t_tr[c] = pe.do(lambda e, c=c, k=k: e.transpose(PB[4 + c % 2][:, k * P:k * P + P],
                                                                    HIN[c % 4][:, k * P:k * P + P], ident))
                ac.on(t_tr[c], t_mm.get(c - 4))
                t_ht[c] = ac.do(lambda e, c=c: e.activation(HT[c % 4], PB[4 + c % 2][:, 0:D], ACT.Copy))
            b = c - 1
            if 0 <= b < NC:
                pe.on(t_ht[b], t_win, t_ev, t_x1.get(b - 2))
                for k in range(2):
                    t_mm[b] = pe.do(lambda e, b=b, k=k: e.matmul(PB[6 + b % 2][:, 0:D], HT[b % 4][:, k * P:k * P + P],
                                                                 Win[:, k, :], start=k == 0, stop=k == 1))
            b = c - 2
            if 0 <= b < NC:
                ve.on(t_mm[b], t_dg[b], t_tg)
                t = ve.do(lambda e, b=b: e.tensor_tensor(DG[b % 4], PB[6 + b % 2][:, 0:D], DG[b % 4], ALU.add))
                ve.on(t)
                t_x1[b] = ve.do(lambda e, b=b: e.scalar_tensor_tensor(X[:, b, :], DG[b % 4], tg[:, 0:1], X[:, b, :],
                                                                      ALU.mult, ALU.add))
                t_st[b] = stats(b, t_x1[b])

        def cols(v, n):
            return v.rearrange("p (c e) -> p c e", e=n)

        def route(picks, logits_at, rb, nt, after):
            cc = NC * picks
            l3, a3 = cols(lg, E), cols(la, E)
            ve.on(after)
            link(ve, lambda e: e.tensor_tensor(l3, logits_at, rb.unsqueeze(1).broadcast_to([P, NC, E]), ALU.add))
            iota = CT[:, C_IO8:C_IO8 + E].unsqueeze(1).broadcast_to([P, NC, E])
            oh = OH[:, 0:E * cc].rearrange("p (e c) -> p c e", e=E)

            def pick(k, m):
                link(ve, lambda e: e.tensor_reduce(m, l3, AX.X, ALU.max))
                link(ve, lambda e: e.tensor_tensor(a3, l3, m.unsqueeze(2).broadcast_to([P, NC, E]), ALU.is_lt))
                link(ve, lambda e: e.scalar_tensor_tensor(a3, a3, 100.0, iota, ALU.mult, ALU.add))
                link(ve, lambda e: e.tensor_reduce(tt, a3, AX.X, ALU.min))
                link(ve, lambda e: e.tensor_tensor(oh[:, k * NC:(k + 1) * NC, :], iota,
                                                   tt.unsqueeze(2).broadcast_to([P, NC, E]), ALU.is_equal))

            pick(0, m1)
            if picks == 1:
                t = link(ve, lambda e: e.tensor_tensor(a3, l3, m1.unsqueeze(2).broadcast_to([P, NC, E]), ALU.subtract))
                ac.on(t)
                t = ac.do(lambda e: e.activation(la, la, ACT.Exp))
                ve.on(t)
                link(ve, lambda e: e.tensor_reduce(pr[:, 0:NC], a3, AX.X, ALU.add))
                link(ve, lambda e: e.reciprocal(pr[:, 0:NC], pr[:, 0:NC]))
            else:
                link(ve, lambda e: e.scalar_tensor_tensor(l3, oh[:, 0:NC, :], -3.0e38, l3, ALU.mult, ALU.add))
                pick(1, m2)
                t = link(ve, lambda e: e.tensor_tensor(tt, m2, m1, ALU.subtract))
                ac.on(t)
                t = ac.do(lambda e: e.activation(tt, tt, ACT.Exp))
                ve.on(t)
                link(ve, lambda e: e.tensor_scalar(m1, tt, 1.0, None, ALU.add))
                link(ve, lambda e: e.reciprocal(pr[:, 0:NC], m1))
                link(ve, lambda e: e.tensor_tensor(pr[:, NC:2 * NC], pr[:, 0:NC], tt, ALU.mult))
            gate = 2 if picks == 1 else 3
            link(ve, lambda e: e.tensor_scalar(pr[:, 0:cc], pr[:, 0:cc], tg[:, gate:gate + 1], None, ALU.mult))
            n = E * cc
            pe.on((ve.sem, ve.n))
            pe.do(lambda e: e.matmul(PB[4][:, 0:n], CT[:, C_U:C_U + P], OH[:, 0:n], start=True, stop=True))
            t = pe.do(lambda e: e.matmul(PB[5][:, 0:n], ones, OH[:, 0:n], start=True, stop=True))
            ve.on(t)
            seg = CT[:, C_SEG:C_SEG + n] if picks == 2 else CT[:, C_SEG16:C_SEG16 + n]
            link(ve, lambda e: e.tensor_tensor_scan(inc[:, 0:n], seg, PB[5][:, 0:n], 0.0, ALU.mult, ALU.add))
            link(ve, lambda e: e.tensor_tensor(rk[:, 0:n], inc[:, 0:n], PB[5][:, 0:n], ALU.subtract))
            link(ve, lambda e: e.tensor_tensor(rk[:, 0:n], rk[:, 0:n], PB[4][:, 0:n], ALU.add))
            last = inc[:, 0:n].rearrange("p (e c) -> p e c", e=E)[:, :, cc - 1]
            link(ve, lambda e: e.tensor_scalar(ntii, last, float(P - 1), None, ALU.add))
            link(ve, lambda e: e.tensor_single_scalar(ntii, ntii, 7, ALU.arith_shift_right))
            link(ve, lambda e: e.tensor_scalar(nti, ntii, 1.0, None, ALU.max))
            link(ve, lambda e: e.tensor_tensor_scan(bi, ones[:, 0:E], nti, 0.0, ALU.mult, ALU.add))
            link(ve, lambda e: e.tensor_tensor(bas, bi, nti, ALU.subtract))
            link(ve, lambda e: e.tensor_scalar(bas, bas, float(P), None, ALU.mult))
            r3 = rk[:, 0:n].rearrange("p (e c) -> p e c", e=E)
            link(ve, lambda e: e.tensor_tensor(r3, r3, bas.unsqueeze(2).broadcast_to([P, E, cc]), ALU.add))
            link(ve, lambda e: e.tensor_tensor(rk[:, 0:n], rk[:, 0:n], OH[:, 0:n], ALU.mult))
            link(ve, lambda e: e.tensor_reduce(pos[:, 0:cc], rk[:, 0:n].rearrange("p (e c) -> p c e", e=E), AX.X, ALU.add))
            t_pos = link(ve, lambda e: e.tensor_copy(posi[:, 0:cc], pos[:, 0:cc]))
            b7 = sc7[:, 0:nt * 7].rearrange("p (t e) -> p t e", e=7)
            link(ve, lambda e: e.tensor_tensor(b7, CT[:, C_IOT:C_IOT + nt].unsqueeze(2).broadcast_to([P, nt, 7]),
                                               bi[:, 0:7].unsqueeze(1).broadcast_to([P, nt, 7]), ALU.is_ge))
            link(ve, lambda e: e.tensor_reduce(mxx[:, 0:nt], b7, AX.X, ALU.add))
            t_eid = link(ve, lambda e: e.tensor_copy(eidi[:, 0:nt], mxx[:, 0:nt]))
            return t_pos, t_eid


        def scatter(c, xnt, xs, t_xn, picks, dst):
            po.on(t_xn)
            for k in range(picks):
                j = k * NC + c
                t = po.dma(dst, lambda e, j=j: e.indirect_dma_start(
                    xs, bass.IndirectOffsetOnAxis(ap=posi[:, j:j + 1].bitcast(U32), axis=0), xnt, None))
            return t

        XN = [WS[1][:, 256 * i:256 * i + 256] for i in range(4)]
        XT = [WS[1][:, 1024 + 256 * i:1280 + 256 * i] for i in range(4)]
        ve.on(inv_std(t_st[NC - 1]))
        t_xn, t_tr, t_xt, t_mm = {}, {}, {}, {}
        for c in range(NC + 1):
            if c < NC:
                ve.on(t_tr.get(c - 4))
                t_xn[c] = ve.do(lambda e, c=c: e.tensor_scalar(XN[c % 4], X[:, c, :], mean[:, c:c + 1],
                                                               rst[:, c:c + 1], ALU.subtract, ALU.mult))
                pe.on(t_xn[c], t_xt.get(c - 2))
                for k in range(2):
                    t_tr[c] = pe.do(lambda e, c=c, k=k: e.transpose(PB[4 + c % 2][:, k * P:k * P + P],
                                                                    XN[c % 4][:, k * P:k * P + P], ident))
                ac.on(t_tr[c], t_mm.get(c - 4))
                t_xt[c] = ac.do(lambda e, c=c: e.activation(XT[c % 4], PB[4 + c % 2][:, 0:D], ACT.Copy))
            b = c - 1
            if 0 <= b < NC:
                pe.on(t_xt[b], t_x1[NC - 1])
                for k in range(2):
                    t_mm[b] = pe.do(lambda e, b=b, k=k: e.matmul(PB[6][:, b * E:b * E + E],
                                                                 XT[b % 4][:, k * P:k * P + P],
                                                                 rw0s[:, k * E:k * E + E], start=k == 0, stop=k == 1))
        t_pos, t_eid = route(1, PB[6][:, 0:NC * E].rearrange("p (c e) -> p c e", e=E), rb0s, NT0, t_mm[NC - 1])

        d_sc = [dsem(f"d_sc{i}") for i in range(4)]
        t_sct = {}
        po.on(t_pos, t_zero)
        for c in range(NC):
            ve.on(t_tr[NC - 1], t_sct.get(c - 4))
            t = ve.do(lambda e, c=c: e.tensor_scalar(XN[c % 4], X[:, c, :], mean[:, c:c + 1],
                                                     rst[:, c:c + 1], ALU.subtract, ALU.mult))
            t_sct[c] = scatter(c, XN[c % 4], xs0, t, 1, d_sc[c % 4])
        t_scat = [t_sct[c] for c in range(NC - 4, NC)]

        ve.on(t_k)
        link(ve, lambda e: e.tensor_scalar(mb[:, 0:NK], mski, -MASKED, MASKED, ALU.mult, ALU.add))
        link(ve, lambda e: e.tensor_scalar(mb[:, 0:NK], mb[:, 0:NK], attb[:, 0:1], None, ALU.add))
        link(ve, lambda e: e.tensor_tensor(mb[:, 12:13], mb[:, 12:13], CT[:, C_PAD:C_PAD + 1], ALU.add))
        link(ve, lambda e: e.tensor_copy(MBH[:, 0:NK], mb))
        t_mbh = link(ve, lambda e: e.tensor_tensor(MBH[:, NK:2 * NK], mb, MBH[:, 0:NK].bitcast(F32), ALU.subtract))
        link(ve, lambda e: e.tensor_copy(ssk, mski))
        t = link(ve, lambda e: e.tensor_reduce(flag[:, 0:1], ssk, AX.X, ALU.max))
        pe.on(t)
        t = pe.do(lambda e: e.matmul(PB[4][0:1, 0:P], flag[:, 0:1], ident, start=True, stop=True))
        ve.on(t)
        t = link(ve, lambda e: e.tensor_reduce(flag[0:1, 1:2], PB[4][0:1, 0:P], AX.X, ALU.max))
        pe.on(t)
        t = pe.do(lambda e: e.matmul(PB[4][:, 0:1], CT[0:1, C_ONE:C_ONE + P], flag[0:1, 1:2], start=True, stop=True))
        ve.on(t)
        t_flag = link(ve, lambda e: e.tensor_scalar(flag[:, 2:3], PB[4][:, 0:1], 32.0 ** -0.5, None, ALU.mult))

        t_kst, t_kev = {}, []

        def keys_a(c):
            a = AK[c % 2]
            k3 = CK[:, c, :].rearrange("p (h d) -> p h d", h=E)
            ve.on(t_kst.get(c - 2), t_au, t_mbh)
            t = ve.do(lambda e: e.tensor_copy(a[:, :, 0:32], k3))
            ve.do(lambda e: e.tensor_copy(a[:, :, 32:64], k3))
            for j, o in ((0, 96), (1, 98)):
                ve.do(lambda e, j=j, o=o: e.tensor_copy(
                    a[:, :, o:o + 1],
                    MBH[:, j * NK + c:j * NK + c + 1].bitcast(F32).unsqueeze(1).broadcast_to([P, E, 1])))
            ve.on(t)
            return ve.do(lambda e: e.tensor_tensor(a[:, :, 64:96], k3, a[:, :, 0:32].bitcast(F32), ALU.subtract))

        t_trf = [t_flag, t_flag]
        trn = [0]
        RB = [4, 5]

        def turn(ins, after, evac, free=None):
            j = trn[0] % len(RB)
            trn[0] += 1
            bank = PB[RB[j]]
            pe.on(*after, t_trf[j])
            for i, v in enumerate(ins):
                t = pe.do(lambda e, i=i, v=v: e.transpose(bank[:, i * P:i * P + P], v, ident), count=i == len(ins) - 1)
            t_trf[j] = evac(bank, t)
            return t, t_trf[j]

        d_w1 = [dsem(f"d_w1{i}") for i in range(2)]
        d_w2 = [dsem(f"d_w2{i}") for i in range(2)]
        d_b = [dsem(f"d_b{i}") for i in range(2)]
        d_xl = [dsem(f"d_xl{i}") for i in range(2)]
        d_y = [dsem(f"d_y{i}") for i in range(2)]

        FXL = [Z0[:, 256 * i:256 * i + 256] for i in range(2)]
        FXT = [Z0[:, 512 + 256 * i:768 + 256 * i] for i in range(2)]
        FS = [Z0[:, 1024 + 512 * i:1536 + 512 * i] for i in range(2)]
        FHT = [Z0[:, 2048 + 512 * i:2560 + 512 * i] for i in range(2)]
        FY = [Z0[:, 3072 + 256 * i:3328 + 256 * i] for i in range(2)]
        FB = [Z0[:, 3584 + 256 * i:3840 + 256 * i] for i in range(2)]

        def experts(layer, nt, xs, ys, w_up, w_down, t_ready, extra, t_eid):
            up_n = 2 * FF if layer == 0 else FF
            t_xl, t_xt, t_xtr, t_up, t_s, t_h, t_ht, t_htr, t_dn, t_y, t_yd, t_w = ({} for _ in range(12))
            regs = {}
            sp.on(t_eid)

            def load_up(i):
                sl = i % 2
                sp.on(t_up.get(2 * (i - 2) + 1))

                def up(e):
                    regs[i] = e.value_load(eidi[0:1, i:i + 1], min_val=0, max_val=E - 1)
                    return e.dma_start(WS[sl][:, 0:2 * up_n].rearrange("p (k n) -> p k n", k=2),
                                       w_up[bass.ds(regs[i] * D, D), :].rearrange("(k p) n -> p k n", p=P))

                t_w[i] = [sp.dma(d_w1[sl], up)]

            def load_down(i):
                sl = i % 2
                sp.on(t_dn.get(2 * (i - 2) + 1))
                t_w[i].append(sp.dma(d_w2[sl], lambda e: e.dma_start(
                    WS[sl][:, 4096:6144].rearrange("p (c n) -> p c n", c=8),
                    w_down[bass.ds(regs[i] * FF, FF), :].rearrange("(c p) n -> p c n", p=P))))
                if layer == 1:
                    sp.on(t_y.get(i - 2), t_ht.get(2 * (i - 2) + 1))
                    sp.dma(d_b[sl], lambda e: e.dma_start(b1c[sl], b11[bass.ds(regs[i] * P, P), :]))
                    t_w[i].append(sp.dma(d_b[sl], lambda e: e.dma_start(
                        FB[sl], b12[bass.ds(regs[i], 1), :].partition_broadcast(P))))

            def load_x(i):
                sp.on(t_xtr.get(i - 2))
                t_xl[i] = load(sp, d_xl[i % 2], FXL[i % 2], xs[i * P:(i + 1) * P, :])

            def turn_x(i):
                def evac(bank, t):
                    ac.on(t, t_up.get(2 * (i - 2) + 1))
                    return ac.do(lambda e: e.activation(FXT[i % 2], bank[:, 0:D], ACT.Copy))

                t_xtr[i], t_xt[i] = turn([FXL[i % 2][:, k * P:k * P + P] for k in range(2)], [t_xl[i]], evac)
                if i + 2 < nt:
                    load_x(i + 2)

            def up(c):
                i, n = divmod(c, 2)
                w = WS[i % 2][:, 0:2 * up_n].rearrange("p (k n) -> p k n", k=2)
                pe.on(t_xt[i], t_w[i][0], t_h.get(c - 2))
                parts = ((0, n * 512), (1, FF + n * 512)) if layer == 0 else ((0, n * 512),)
                for b, o in parts:
                    for k in range(2):
                        t = pe.do(lambda e, b=b, o=o, k=k: e.matmul(
                            PB[2 * (c % 2) + b], FXT[i % 2][:, k * P:k * P + P], w[:, k, o:o + 512],
                            start=k == 0, stop=k == 1), count=k == 1)
                t_up[c] = t
                a, g = PB[2 * (c % 2)], PB[2 * (c % 2) + 1]
                s = FS[c % 2]
                if layer == 0:
                    ac.on(t, t_htr.get(c - 2))
                    t_s[c] = ac.do(lambda e: e.activation(s, a, ACT.Silu))
                    ve.on(t_s[c])
                    t_h[c] = ve.do(lambda e: e.tensor_tensor(s, s, g, ALU.mult))
                else:
                    ve.on(t, t_htr.get(c - 2))
                    t_h[c] = ve.do(lambda e: e.tensor_copy(s, a))

            def turn_h(c):
                i, n = divmod(c, 2)

                def evac(bank, t):
                    ac.on(t, t_dn.get(c - 2))
                    if layer == 0:
                        return ac.do(lambda e: e.activation(FHT[c % 2], bank, ACT.Copy))
                    ac.on(t_w[i][2])
                    for j in range(4):
                        r = ac.do(lambda e, j=j: e.activation(FHT[c % 2][:, j * P:j * P + P], bank[:, j * P:j * P + P],
                                                              ACT.Silu, bias=b1c[i % 2][:, 4 * n + j:4 * n + j + 1]))
                    return r

                t_htr[c], t_ht[c] = turn([FS[c % 2][:, j * P:j * P + P] for j in range(4)], [t_h[c]], evac)

            def down(c):
                i, n = divmod(c, 2)
                w = WS[i % 2][:, 4096:6144].rearrange("p (c n) -> p c n", c=8)
                y = PB[6 + i % 2][:, 0:D]
                pe.on(t_ht[c], t_w[i][1], t_y.get(i - 2))
                for j in range(4):
                    t_dn[c] = pe.do(lambda e, j=j: e.matmul(y, FHT[c % 2][:, j * P:j * P + P], w[:, 4 * n + j, :],
                                                            start=n == 0 and j == 0, stop=n == 1 and j == 3),
                                    count=j == 3)
                if n == 1:
                    ve.on(t_dn[c], t_yd.get(i - 2))
                    if layer == 0:
                        t_y[i] = ve.do(lambda e: e.tensor_copy(FY[i % 2], y))
                    else:
                        ve.on(t_w[i][2])
                        t_y[i] = ve.do(lambda e: e.tensor_tensor(FY[i % 2], y, FB[i % 2], ALU.add))
                    if i + 2 < nt:
                        load_down(i + 2)
                    sp.on(t_y[i])
                    t_yd[i] = load(sp, d_y[i % 2], ys[i * P:(i + 1) * P, :], FY[i % 2])

            sp.on(*t_ready)
            for i in range(2):
                load_x(i)
                load_up(i)
                load_down(i)
            turn_x(0)
            for c in range(2 * nt + 2):
                if c < 2 * nt:
                    up(c)
                    if c % 2 and c // 2 + 2 < nt:
                        load_up(c // 2 + 2)
                if 1 <= c <= 2 * nt:
                    turn_h(c - 1)
                if c % 2 == 0 and c // 2 + 1 < nt:
                    turn_x(c // 2 + 1)
                if c >= 2:
                    down(c - 2)
                extra(c)
            return [t_yd[nt - 2], t_yd[nt - 1]], t_dn[2 * nt - 1]

        def keys_b(c, t_a):
            for f in range(2):
                def evac(bank, t, f=f):
                    ac.on(t)
                    return ac.do(lambda e: e.activation(
                        KS[:, 4 * f:4 * f + 4, c * P:c * P + P], bank.rearrange("p (h k) -> p h k", h=4), ACT.Copy))

                t_kst[c], r = turn([AK[c % 2][:, 4 * f + h, :].bitcast(F32) for h in range(4)], [t_a], evac)
            t_kev.append(r)

        def keys(c):
            if c % 2 == 1 and 1 <= c // 2 + 1 <= NK:
                keys_b(c // 2, keys_a(c // 2))

        t_yd, t_last = experts(0, NT0, xs0, ys0, w01, w02,
                               [*t_scat, t_zero, t_zero1, t_pos, t_x1[NC - 1], t_tr[NC - 1], t_pq], keys, t_eid)

        GR = [Z1[:, 256 * i:256 * i + 256] for i in range(8)]
        d_gr = [dsem(f"d_gr{i}") for i in range(8)]
        t_x2 = {}
        po.on(*t_yd, *t_kst.values())
        po.on((ve.sem, ve.n))
        t_y = {}

        def fetched(g):
            for c in range(4 * g, 4 * g + 4):
                po.on(t_x2.get(c - 8))
                t_y[c] = po.dma(d_gr[c % 8], lambda e, c=c: e.indirect_dma_start(
                    GR[c % 8], None, ys0, bass.IndirectOffsetOnAxis(ap=posi[:, c:c + 1].bitcast(U32), axis=0)))

        def added(g):
            for c in range(4 * g, 4 * g + 4):
                ve.on(t_y[c])
                t_x2[c] = ve.do(lambda e, c=c: e.scalar_tensor_tensor(
                    X[:, c, :], GR[c % 8], pr[:, c:c + 1], X[:, c, :], ALU.mult, ALU.add))
                t = stats(c, t_x2[c])
            return t

        def query_norms(t, a, b):
            ve.on(t)
            link(ve, lambda e: e.tensor_scalar(rst2[:, a:b], rst[:, a:b], flag[:, 2:3], None, ALU.mult))

        fetched(0)
        fetched(1)
        query_norms(inv_std(added(0), 0, 4), 0, 4)

        RW1 = Z0[:, 0:2048].rearrange("p (k n) -> p k n", k=2)
        d_rw = dsem("d_rw")
        sp.on(t_last, (ve.sem, ve.n), (ac.sem, ac.n))
        t_rw = load(sp, d_rw, RW1, rw1.rearrange("(k p) n -> p k n", p=P))
        QT = [Z0[:, 2048 + 128 * i:2176 + 128 * i] for i in range(2)]
        REC, OT = Z0[:, 2304:2816], Z0[:, 2816:3328]
        MP = [Z0[:, 3328 + 16 * i:3344 + 16 * i] for i in range(2)]
        MX, NM = Z0[:, 3360:3364], Z0[:, 3364:3368]
        RT = Z0[:, 3368:3384]
        PT = [Z1[:, 512 * i:512 * i + 512] for i in range(8)]
        RB.append(3)
        t_trf.append(None)
        t_red = [None]
        RB3 = (4, 5, 3)
        PIECE = NK * P // 4
        ring = trn
        t_qs, t_aq = {}, {}
        t_qfree = {}
        t_at = {}
        t_aut = {}
        qn = [0]

        def queries(n, t4):
            qg, hf = divmod(n, 2)
            c = 4 * qg + t4
            j = qn[0]
            qn[0] += 1
            a = AK[j % 2]
            qt = QT[j % 2]
            q3 = qt.rearrange("p (h d) -> p h d", h=4)
            ve.on(t_aq.get(j - 2), *t_kst.values())
            t = ve.do(lambda e: e.tensor_scalar(
                qt, X[:, c, hf * P:hf * P + P], mean[:, c:c + 1], rst2[:, c:c + 1], ALU.subtract, ALU.mult))
            if j < 2:
                for o, v in ((96, 1.0), (97, 0.0), (98, 1.0), (99, 0.0)):
                    ve.do(lambda e, o=o, v=v: e.memset(a[:, 0:4, o:o + 1].bitcast(F32), v))
            ve.on(t)
            t = ve.do(lambda e: e.tensor_copy(a[:, 0:4, 0:32], q3))
            ve.do(lambda e: e.tensor_copy(a[:, 0:4, 64:96], q3))
            ve.on(t)
            return j, ve.do(lambda e: e.tensor_tensor(a[:, 0:4, 32:64], q3, a[:, 0:4, 0:32].bitcast(F32), ALU.subtract))

        def turn_q(n, t4, j, t):
            q = QS[n % 2]

            def evac(bank, tt_):
                ac.on(tt_, t_qfree.get(n - 2))
                return ac.do(lambda e: e.activation(q[:, :, t4 * P:t4 * P + P],
                                                    bank.rearrange("p (h k) -> p h k", h=4), ACT.Copy))

            t_aq[j], t_q = turn([AK[j % 2][:, h, :].bitcast(F32) for h in range(4)], [t], evac)
            return t_q

        def negated(mp, j):
            au = AU[j % 2]
            ve.on(t_red[0], t_aut.get(j - 2), t_au)
            t = ve.do(lambda e: e.tensor_reduce(MX, mp.rearrange("p (h s) -> p h s", s=4), AX.X, ALU.max))
            ve.on(t)
            t = ve.do(lambda e: e.tensor_scalar(NM, MX, -1.0, None, ALU.mult))
            ve.on(t)
            t = ve.do(lambda e: e.tensor_copy(au[:, :, 97:98], NM.unsqueeze(2)))
            ve.on(t)
            return ve.do(lambda e: e.tensor_tensor(au[:, :, 99:100], NM.unsqueeze(2),
                                                   au[:, :, 97:98].bitcast(F32), ALU.subtract))

        def turn_m(n, t4, j, t):
            q = QS[n % 2]

            def evac(bank, tt_):
                ac.on(tt_, t_red[0])
                return ac.do(lambda e: e.activation(
                    q[96:128, :, t4 * P:t4 * P + P], bank[96:128, :].rearrange("p (h k) -> p h k", h=4), ACT.Copy))

            t_aut[j], t_qs[n] = turn([AU[j % 2][:, h, :].bitcast(F32) for h in range(4)], [t], evac)

        def maxima(n):
            hf = n % 2
            q = QS[n % 2]
            j, t = queries(n, 0)
            yield
            t_q = turn_q(n, 0, j, t)
            held = None
            for t4 in range(4):
                mp = MP[j % 2]
                for h in range(4):
                    for s in range(4):
                        b = ring[0] % 3
                        ring[0] += 1
                        pe.on(t_q, t_trf[b])
                        t = pe.do(lambda e, h=h, s=s, b=b, t4=t4: e.matmul(
                            PB[RB3[b]][:, 0:PIECE], q[:, h, t4 * P:t4 * P + P],
                            KS[:, 4 * hf + h, s * PIECE:(s + 1) * PIECE], start=True, stop=True))
                        ve.on(t)
                        t_trf[b] = ve.do(lambda e, h=h, s=s, b=b, mp=mp: e.tensor_reduce(
                            mp[:, 4 * h + s:4 * h + s + 1], PB[RB3[b]][:, 0:PIECE], AX.X, ALU.max))
                        t_red[0] = t_trf[b]
                        if 4 * h + s == 4 and held:
                            turn_m(n, *held)
                        if 4 * h + s == 8 and t4 < 3:
                            nxt = queries(n, t4 + 1)
                        if 4 * h + s == 13 and t4 < 3:
                            t_qn = turn_q(n, t4 + 1, *nxt)
                        yield
                held = (t4, j, negated(mp, j))
                if t4 < 3:
                    j, t_q = nxt[0], t_qn
            yield
            yield
            turn_m(n, *held)
            yield

        t_bank = [None, None, None]
        t_pt = {}
        pairs = [0]
        t_x3 = {}

        exps, t_pp, t_acc = {}, {}, {}
        ACC = [WS[i][:, 0:2048] for i in range(2)]
        t_ppl = {}

        def scores(n, kc, hh):
            hf = n % 2
            g = pairs[0]
            pairs[0] += 1
            pe.on(t_qs[n], *t_kev, t_bank[g % 3])
            t = pe.do(lambda e: e.matmul(PB[g % 3], KS[:, 4 * hf + hh, kc * P:kc * P + P], QS[n % 2][:, hh, :],
                                         start=True, stop=True))
            ac.on(t, t_pt.get(g - 8), t_pp.get(g - 8), t_x2[NC - 1])
            t_bank[g % 3] = ac.do(lambda e: e.activation(PT[g % 8], PB[g % 3], ACT.Exp))
            exps[(n, kc, hh)] = (g, t_bank[g % 3])
            if kc == NK - 1:
                t_qfree[n] = t
            if kc % 2 == 0:
                acc = ACC[n % 2][:, 512 * hh:512 * hh + 512]
                po.on(t_bank[g % 3])
                if kc == 0:
                    po.on(t_acc.get((n - 2, hh)), t_ppl.get((n - 2, hh)))
                    t_pp[g] = po.do(lambda e: e.tensor_copy(acc, PT[g % 8]))
                else:
                    po.on(t_pp[exps[(n, kc - 2, hh)][0]])
                    t_pp[g] = po.do(lambda e: e.tensor_tensor(acc, acc, PT[g % 8], ALU.add))
                t_ppl[(n, hh)] = t_pp[g]

        def values(n, kc, bank):
            hf = n % 2
            for hh in range(4):
                pe.on(exps[(n, kc, hh)][1])
            if kc == 0:
                pe.on(t_last, t_yd[1], *t_at.get(n - 1, ()))
            if bank == 7 and kc % 2 == 0 and kc < NK - 1:
                return
            for hh in range(4):
                g = exps[(n, kc, hh)][0]
                src = PT[g % 8]
                if bank == 7 and kc == NK - 1:
                    pe.on(t_pp[g])
                    src = ACC[n % 2][:, 512 * hh:512 * hh + 512]
                lhs = V[:, kc, (4 * hf + hh) * 32:(4 * hf + hh) * 32 + 32] if bank == 6 else ones[:, 0:32]
                t_pt[g] = pe.do(lambda e, lhs=lhs, hh=hh, src=src: e.matmul(
                    PB[bank][32 * hh:32 * hh + 32, :], lhs, src, start=kc == bank - 6,
                    stop=kc == NK - 1, tile_position=(0, 32 * hh)))
                if bank == 7 and kc == NK - 1:
                    t_acc[(n, hh)] = t_pt[g]

        def attended(n):
            qg, hf = divmod(n, 2)
            t_done = (pe.sem, pe.n)
            ve.on(t_done, t_x3.get('r'))
            t_r = ve.do(lambda e: e.tensor_copy(REC, PB[7]))
            ac.on(t_done, t_x3.get("t"))
            t_o_ = ac.do(lambda e: e.activation(OT, PB[6], ACT.Copy))
            t_at[n] = (t_r, t_o_)

            def into_x():
                def evac_r(bank, tt_):
                    ve.on(tt_)
                    return ve.do(lambda e: e.reciprocal(RT, bank.rearrange("p (g d) -> p g d", d=32)[:, :, 0]))

                t_x3["r"], t_rt = turn([REC[:, j * P:j * P + P] for j in range(4)], [t_r], evac_r)

                def evac(bank, tt_):
                    ve.on(tt_, t_rt)
                    return ve.do(lambda e: e.tensor_tensor(
                        OT.rearrange("p (g d) -> p g d", d=32), bank.rearrange("p (g d) -> p g d", d=32),
                        RT.unsqueeze(2).broadcast_to([P, 16, 32]), ALU.mult))

                _, t = turn([OT[:, j * P:j * P + P] for j in range(4)], [t_o_], evac)
                ve.on(t)
                v = X[:, 4 * qg:4 * qg + 4, hf * P:hf * P + P]
                t_x3["t"] = t_x3[n] = ve.do(lambda e: e.scalar_tensor_tensor(
                    v, OT.rearrange("p (c d) -> p c d", c=4), tg[:, 1:2], v, ALU.mult, ALU.add))

            late.append(into_x)

        late = []
        pe.on(*t_yd)
        for i, _ in enumerate(maxima(0)):
            if i in (8, 20, 32):
                g = (i + 4) // 12
                if g < 3:
                    fetched(g + 1)
                t = added(g)
                if g == 3:
                    t = inv_std(t, 4, NC)
        query_norms(t, 4, NC)
        side = iter(())
        for step in range(8 * NK + 1):
            n, kc = divmod(step, NK)
            if kc == 0:
                for _ in side:
                    pass
                side = maxima(n + 1) if n < 7 else iter(())
            for half in range(2):
                if n < 8:
                    scores(n, kc, 2 * half)
                    scores(n, kc, 2 * half + 1)
                    next(side, None)
                if step:
                    m, j = divmod(step - 1, NK)
                    values(m, j, 6 + half)
                    next(side, None)
                    next(side, None)
            if step and j == NK - 1:
                attended(m)
            if kc == 3 and late:
                late.pop()()
                if n == 7:
                    for c in range(NC - 4):
                        stats(c, t_x3[5])
        late.pop()()

        for c in range(NC - 4, NC):
            t = stats(c, t_x3[7])
        ve.on(inv_std(t))
        XR = [Z1[:, 256 * i:256 * i + 256] for i in range(4)]
        XG = [Z1[:, 1024 + 1024 * i:2048 + 1024 * i].rearrange("p (k q) -> p k q", k=2) for i in range(2)]
        HR = [Z1[:, 3072 + 512 * i:3584 + 512 * i] for i in range(2)]
        LT = Z0[0:8, 2048:2560]
        t_xn, t_xtr, t_xg, t_hb, t_hr, t_lm, t_rb = {}, {}, {}, {}, {}, {}, {}
        ve.on(t_pt[pairs[0] - 1])
        t_lt = None
        for g in range(4):
            for t4 in range(4):
                c = 4 * g + t4
                ve.on(t_xtr.get(c - 4))
                t_xn[c] = ve.do(lambda e, c=c: e.tensor_scalar(XR[c % 4], X[:, c, :], mean[:, c:c + 1],
                                                               rst[:, c:c + 1], ALU.subtract, ALU.mult))

                def evac(bank, t, g=g, t4=t4):
                    ve.on(t, t_rb.get(8 * (g - 2) + 7))
                    return ve.do(lambda e: e.tensor_copy(XG[g % 2][:, :, t4 * P:t4 * P + P],
                                                         bank[:, 0:D].rearrange("p (k q) -> p k q", k=2)))

                t_xtr[c], t_xg[g] = turn([XR[c % 4][:, k * P:k * P + P] for k in range(2)], [t_xn[c]], evac)
            for f in range(9):
                if f < 8:
                    m = 8 * g + f
                    pe.on(t_xg[g], t_rw, t_hr.get(m - 3), *t_bank, *t_at[7])
                    for k in range(2):
                        t_rb[m] = pe.do(lambda e, k=k, m=m, f=f, g=g: e.matmul(
                            PB[m % 3], RW1[:, k, f * P:f * P + P], XG[g % 2][:, k, :], start=k == 0, stop=k == 1))
                    ac.on(t_rb[m], t_lm.get(m - 2))
                    t_hr[m] = ac.do(lambda e, m=m, f=f: e.activation(HR[m % 2], PB[m % 3], ACT.Silu,
                                                                     bias=rb1s[:, f:f + 1]))
                if f >= 1:
                    m = 8 * g + f - 1
                    pe.on(t_hr[m], t_lt)
                    t_lm[m] = pe.do(lambda e, m=m, f=f: e.matmul(PB[6][0:8, :], rw2s[:, 8 * f - 8:8 * f], HR[m % 2],
                                                                 start=f == 1, stop=f == 8))
            ve.on(t_lm[8 * g + 7], t_x3.get(("l", g - 1)))
            t_lt = ve.do(lambda e: e.tensor_copy(LT, PB[6][0:8, :]))
            pe.on(t_lt)
            for t4 in range(4):
                c = 4 * g + t4
                t_x3[("l", g)] = pe.do(lambda e, c=c, t4=t4: e.transpose(PB[7][:, c * E:c * E + E],
                                                                         LT[:, t4 * P:t4 * P + P], ident[0:8, 0:8]))
        pe.on(t_trf[0], t_trf[1])
        t_pos, t_eid = route(2, PB[7][:, 0:NC * E].rearrange("p (c e) -> p c e", e=E), rb2s, NT1, t_x3[("l", 3)])

        t_sct = {}
        po.on(t_pos, t_zero1)
        ve.on(t_xtr[NC - 1])
        for c in range(NC):
            ve.on(t_sct.get(c - 4))
            t = ve.do(lambda e, c=c: e.tensor_scalar(XR[c % 4], X[:, c, :], mean[:, c:c + 1],
                                                     rst[:, c:c + 1], ALU.subtract, ALU.mult))
            t_sct[c] = scatter(c, XR[c % 4], xs1, t, 2, d_sc[c % 4])
        t_scat = [t_sct[c] for c in range(NC - 4, NC)]

        RB.pop()
        pe.on(t_trf.pop())
        t_yd, t_last = experts(1, NT1, xs1, ys1, w11, w12, [*t_scat, t_rb[31], (ac.sem, ac.n), (ve.sem, ve.n)],
                               lambda c: None, t_eid)
        po.on(*t_yd)
        t_o = {}
        d_o = dsem("d_o")
        t_free = {}
        for c in range(NC):
            g1, g2 = GR[(2 * c) % 8], GR[(2 * c + 1) % 8]
            for k, g in ((0, g1), (1, g2)):
                po.on(t_free.get(c - 4))
                t = po.dma(d_gr[(2 * c + k) % 8], lambda e, c=c, k=k, g=g: e.indirect_dma_start(
                    g, None, ys1, bass.IndirectOffsetOnAxis(ap=posi[:, k * NC + c:k * NC + c + 1].bitcast(U32), axis=0)))
                ve.on(t)
                t = ve.do(lambda e, c=c, k=k, g=g: e.scalar_tensor_tensor(X[:, c, :], g, pr[:, k * NC + c:k * NC + c + 1],
                                                                         X[:, c, :], ALU.mult, ALU.add))
                ve.on(t)
            t_free[c] = t
            sp.on(t)
            load(sp, d_o, out[c * P:(c + 1) * P, :], X[:, c, :])
        sp.on((d_o.sem, d_o.n))

        block = es.enter_context(nc.Block())

        @block.sync
        def _(e):
            sp.play(e)

        @block.tensor
        def _(e):
            pe.play(e)

        @block.scalar
        def _(e):
            ac.play(e)

        @block.vector
        def _(e):
            ve.play(e)

        @block.gpsimd
        def _(e):
            po.play(e)


def kernel(x, ctx_2048, mask_BxS2_if0, mask_BxS2_ik0, g_xattn, g_ffn, L0_xattn_W_in, L0_xattn_b_in, L0_xattn_g_res,
           L0_xattn_g_init, L0_ffn_router_w, L0_ffn_router_b, L0_ffn_w1, L0_ffn_w2, L1_xattn_b, L1_ffn_rw1,
           L1_ffn_rb1, L1_ffn_rw2, L1_ffn_rb2, L1_ffn_w1, L1_ffn_b1, L1_ffn_w2, L1_ffn_b2):
    import concourse.bacc as bacc
    from concourse.bass_utils import run_bass_kernel_spmd

    def arr(a, *shape):
        return np.ascontiguousarray(np.asarray(a).reshape(shape))

    def by_partition(a, n):
        a = np.asarray(a).reshape(-1)
        r = np.zeros(n * P, a.dtype)
        r[:a.size] = a
        return np.ascontiguousarray(r.reshape(n, P).T)

    ins = {
        "cst": constants(),
        "x": arr(x, T, D),
        "ctx_2048": arr(ctx_2048, S2, 2 * D),
        "plen": by_partition(mask_BxS2_if0, NK),
        "kmask": by_partition(mask_BxS2_ik0, NK),
        "g_xattn": arr(g_xattn, 1, 2),
        "g_ffn": arr(g_ffn, 1, 2),
        "W_in": np.ascontiguousarray(np.asarray(L0_xattn_W_in).T),
        "b_in": arr(L0_xattn_b_in, 1, D),
        "g_res": by_partition(L0_xattn_g_res, 2),
        "g_init": arr(L0_xattn_g_init, 1, 2 * D),
        "rw0": arr(L0_ffn_router_w, D, E),
        "rb0": arr(L0_ffn_router_b, 1, E),
        "w01": arr(L0_ffn_w1, E * D, 2 * FF),
        "w02": arr(L0_ffn_w2, E * FF, D),
        "att_b": arr(L1_xattn_b, 1, 1),
        "rw1": arr(L1_ffn_rw1, D, FF),
        "rb1": by_partition(L1_ffn_rb1, 8),
        "rw2": arr(L1_ffn_rw2, FF, E),
        "rb2": arr(L1_ffn_rb2, 1, E),
        "w11": arr(L1_ffn_w1, E * D, FF),
        "b11": np.ascontiguousarray(np.asarray(L1_ffn_b1).reshape(E, 8, P).transpose(0, 2, 1).reshape(E * P, 8)),
        "w12": arr(L1_ffn_w2, E * FF, D),
        "b12": arr(L1_ffn_b2, E, D),
    }
    nc = bacc.Bacc("TRN2", target_bir_lowering=False, num_devices=1)
    args, arrays = {}, {}
    for name, a in ins.items():
        arrays["in_" + name] = a
        args[name] = nc.dram_tensor("in_" + name, a.shape, mybir.dt.from_np(a.dtype), kind="ExternalInput").ap()
    out = nc.dram_tensor("out_0", (T, D), F32, kind="ExternalOutput").ap()
    build(nc, out=out, **args)
    r = run_bass_kernel_spmd(nc, [arrays], core_ids=[0])
    return np.asarray(r.results[0]["out_0"]).reshape(1, T, D)
```
